# Optimizing a Trainium2 kernel written in Bass

```python
import numpy as np
import jax
import jax.numpy as jnp

def _softmax(x, axis=-1):
    return jax.nn.softmax(x, axis=axis)

def _gelu(x):
    return jax.nn.gelu(x, approximate=True)

def _silu(x):
    return jax.nn.silu(x)

def _sigmoid(x):
    return jax.nn.sigmoid(x)

def _layernorm(x, axis=-1, eps=1e-05):
    m = jnp.mean(x, axis=axis, keepdims=True)
    v = jnp.var(x, axis=axis, keepdims=True)
    return (x - m) / jnp.sqrt(v + eps)

def _scatter_add(tgt, idx, src, axis=0):
    return tgt.at[idx].add(src)

def _segment_sum(src, seg, n):
    return jax.ops.segment_sum(src, seg, n)
kernel_name = 'mk_seq_preln_d1_jaxref_r8_be3f04'

def setup_inputs(seed: int=0):
    np.random.seed(seed)
    _w = jnp.asarray

    def _L0_attn_setup():
        import jax, jax.numpy as jnp
        import numpy as np
        D_INNER, DT_RANK, D_STATE = (256, 64, 16)
        B_SZ, L = (2, 128)
        key = jax.random.key(seed)
        ks = jax.random.split(key, 4)
        x = jax.random.normal(ks[0], (B_SZ, L, D_INNER), dtype=jnp.float32)
        W_xproj = jax.random.normal(ks[1], (DT_RANK + 2 * D_STATE, D_INNER), dtype=jnp.float32) * (1.0 / np.sqrt(D_INNER))
        W_dt = jax.random.normal(ks[2], (D_INNER, DT_RANK), dtype=jnp.float32) * (1.0 / np.sqrt(DT_RANK))
        b_dt = jax.random.normal(ks[3], (D_INNER,), dtype=jnp.float32) * 0.01
        A_log = jnp.log(jnp.broadcast_to(jnp.arange(1, D_STATE + 1, dtype=jnp.float32), (D_INNER, D_STATE)))
        D = jnp.ones((D_INNER,), dtype=jnp.float32)
        return {'x': x, 'W_xproj': W_xproj, 'W_dt': W_dt, 'b_dt': b_dt, 'A_log': A_log, 'D': D}
    _L0_attn_in = _L0_attn_setup()

    def _L0_ffn_setup():
        import jax, jax.numpy as jnp
        import numpy as np
        B, S, D_IN, D_OUT, E = (4, 128, 256, 256, 32)
        MASK_DENSITY = 0.3
        THRESH = 0.5
        key = jax.random.key(seed)
        k_x, k_w, k_m, k_r = jax.random.split(key, 4)
        x = jax.random.normal(k_x, (B, S, D_IN), dtype=jnp.float32)
        bound = np.sqrt(1.0 / D_IN) * np.sqrt(3.0)
        weight = jax.random.uniform(k_w, (D_OUT, D_IN), minval=-bound, maxval=bound, dtype=jnp.float32)
        scale = jnp.ones((D_OUT,), dtype=jnp.float32)
        expert_masks = (jax.random.uniform(k_m, (E, D_OUT, D_IN)) < MASK_DENSITY).astype(jnp.float32)
        router_w = 0.01 * jax.random.normal(k_r, (E, D_IN), dtype=jnp.float32)
        return {'x': x, 'weight': weight, 'scale': scale, 'expert_masks': expert_masks, 'router_w': router_w}
    _L0_ffn_in = _L0_ffn_setup()
    _d = {'L0_attn_x': _L0_attn_in['x'], 'L0_attn_W_xproj': _L0_attn_in['W_xproj'], 'L0_attn_W_dt': _L0_attn_in['W_dt'], 'L0_attn_b_dt': _L0_attn_in['b_dt'], 'L0_attn_A_log': _L0_attn_in['A_log'], 'L0_attn_D': _L0_attn_in['D'], 'L0_ffn_weight': _L0_ffn_in['weight'], 'L0_ffn_scale': _L0_ffn_in['scale'], 'L0_ffn_expert_masks': _L0_ffn_in['expert_masks'], 'L0_ffn_router_w': _L0_ffn_in['router_w']}
    _x0 = _d['L0_attn_x']
    _d['L0_attn_x'] = jax.random.normal(jax.random.fold_in(jax.random.key(seed), 1), (2, 1024, 256), dtype=_x0.dtype)
    del _x0
    return _d

def reference(L0_attn_x, L0_attn_W_xproj, L0_attn_W_dt, L0_attn_b_dt, L0_attn_A_log, L0_attn_D, L0_ffn_weight, L0_ffn_scale, L0_ffn_expert_masks, L0_ffn_router_w):

    def _L0_attn_ref(x, W_xproj, W_dt, b_dt, A_log, D):
        import jax, jax.numpy as jnp
        import numpy as np
        D_INNER, DT_RANK, D_STATE = (256, 64, 16)
        B_SZ, L = (2, 128)
        A = -jnp.exp(A_log)
        x_dbl = jnp.einsum('bld,kd->blk', x, W_xproj)
        delta = x_dbl[..., :DT_RANK]
        Bmat = x_dbl[..., DT_RANK:DT_RANK + D_STATE]
        Cmat = x_dbl[..., DT_RANK + D_STATE:]
        delta = jax.nn.softplus(jnp.einsum('blr,dr->bld', delta, W_dt) + b_dt)
        deltaA = jnp.exp(delta[..., None] * A)
        BX = delta[..., None] * Bmat[:, :, None, :] * x[..., None]
        dA_t = jnp.moveaxis(deltaA, 1, 0)
        BX_t = jnp.moveaxis(BX, 1, 0)
        C_t = jnp.moveaxis(Cmat, 1, 0)
        h0 = jnp.zeros((x.shape[0], D_INNER, D_STATE), dtype=x.dtype)

        def step(h, inp):
            dA, bx, c = inp
            h = dA * h + bx
            y = jnp.einsum('bdn,bn->bd', h, c)
            return (h, y)
        _, ys = jax.lax.scan(step, h0, (dA_t, BX_t, C_t))
        y = jnp.moveaxis(ys, 0, 1) + D * x
        return y

    def _L0_ffn_ref(x, weight, scale, expert_masks, router_w):
        import jax, jax.numpy as jnp
        import numpy as np
        B, S, D_IN, D_OUT, E = (4, 128, 256, 256, 32)
        MASK_DENSITY = 0.3
        THRESH = 0.5
        logits = jnp.einsum('bsd,ed->bse', x, router_w)
        probs = jax.nn.softmax(logits, axis=-1)
        top1_w = jnp.max(probs, axis=-1)
        top1_idx = jnp.argmax(probs, axis=-1)
        w_q = jnp.clip(jnp.round(weight / THRESH), -1.0, 1.0)
        w_scaled = w_q * scale[:, None]
        out0 = jnp.zeros((x.shape[0], x.shape[1], weight.shape[0]), dtype=x.dtype)

        def body(out, inputs):
            e_idx, mask_e = inputs
            y = jnp.einsum('bsi,oi->bso', x, w_scaled * mask_e)
            sel = (top1_idx == e_idx)[..., None]
            out = jnp.where(sel, y * top1_w[..., None], out)
            return (out, None)
        out, _ = jax.lax.scan(body, out0, (jnp.arange(E), expert_masks))
        return out
    x = L0_attn_x
    x = x + _L0_attn_ref(_layernorm(x, axis=-1), L0_attn_W_xproj, L0_attn_W_dt, L0_attn_b_dt, L0_attn_A_log, L0_attn_D)
    x = x + _L0_ffn_ref(_layernorm(x, axis=-1), L0_ffn_weight, L0_ffn_scale, L0_ffn_expert_masks, L0_ffn_router_w)
    return x

_drawn_inputs = setup_inputs


def setup_inputs(seed=0):
    import zlib

    import numpy as np

    out = dict(_drawn_inputs(seed))
    spreads = {'L0_attn_D': (1.0, 0.2), 'L0_ffn_scale': (1.0, 0.2)}
    factors = {'L0_attn_b_dt': 8.0}
    for name, (base, spread) in spreads.items():
        noise = np.random.default_rng([zlib.crc32(name.encode()), seed]).standard_normal(out[name].shape)
        drawn = base * np.exp(spread * noise) if base else spread * noise
        out[name] = jnp.asarray(drawn.astype(out[name].dtype))
    for name, factor in factors.items():
        out[name] = (out[name] * factor).astype(out[name].dtype)
    return out
```

```python
import concourse.bass as bass
from concourse import mybir
from contextlib import ExitStack

P = 128
B, L, D = 2, 1024, 256
R, N = 64, 16
E = 32
T = B * L
TB = T // P
LB = L // P
DH = D // P
HC = 512
LH = L // HC
SLOT_TILES = 48
SLOTS = SLOT_TILES * P
EPS = 1e-5
C_ID, C_TRI, C_ONE, C_RE, C_CNT, C_TILE, C_END = 0, 128, 256, 384, 416, 432, 480


def selective_scan_then_routed_ternary_ffn(nc, x, w_xproj, w_dt, b_dt, a_log, d_skip,
                                           weight, scale, masks, router_w, consts, out):
    fp32, fp16, bf16 = mybir.dt.float32, mybir.dt.float16, mybir.dt.bfloat16
    i32 = mybir.dt.int32
    ALU, ACT, AX = mybir.AluOpType, mybir.ActivationFunctionType, mybir.AxisListType

    xs = nc.dram_tensor("sorted_tokens", (SLOTS, 2 * D), fp16, kind="Internal").ap()
    ys = nc.dram_tensor("sorted_outputs", (SLOTS, D), fp32, kind="Internal").ap()

    ctx = ExitStack()
    with ctx:
        def sb(name, shape, dt=fp32):
            return ctx.enter_context(nc.sbuf_tensor(name, shape, dt))

        def sem(name):
            return ctx.enter_context(nc.semaphore(name))

        cst = sb("cst", [P, C_END])
        ident = cst[:, C_ID:C_ID + P]
        ident16 = sb("ident16", [P, P], fp16)
        tri_bf = sb("tri_bf", [P, P], bf16)
        ones_bf = sb("ones_bf", [P, P], bf16)
        pick = sb("pick", [96, E], bf16)
        x_sb = sb("x_sb", [P, TB, D])
        xn = sb("xn", [P, TB, D])
        xnT = sb("xnT", [P, DH, T])
        delta = sb("delta", [P, DH, T])
        u = sb("u", [P, DH, T])
        yT = xn[:, :, :].rearrange("p t d -> p (t d)").rearrange("p (h l) -> p h l", h=DH)
        bdt = sb("bdt", [P, DH])
        dsk = sb("dsk", [P, DH])
        alog = sb("alog", [P, DH, N])
        a_exp = sb("a_exp", [P, DH, N])
        a_neg = sb("a_neg", [P, DH, N])
        scale_bc = sb("scale_bc", [P, D])
        wxT = sb("wxT", [P, DH, R + 96])
        wdT = sb("wdT", [R, D])
        rwT = sb("rwT", [P, DH, E])
        wqT = sb("wqT", [P, DH, D])
        diag_d = sb("diag_d", [P, DH, P])
        bc3 = sb("bc3", [96, T], bf16)
        st = sb("st", [P, TB, 6])
        mv = sb("mv", [P, TB, 2])
        ve = sb("ve", [P, TB])
        lnv = sb("lnv", [P, TB])
        r0 = sb("r0", [P, TB])
        rr = sb("rr", [P, TB])
        rt = sb("rt", [P, TB])
        rstd = sb("rstd", [P, TB])
        dA = sb("dA", [P, 2, DH, L])
        bx = sb("bx", [P, DH, L])
        h = sb("h", [P, 2, DH, L])
        prod = sb("prod", [P, 2, DH, L])
        cb = sb("cb", [P, 2, L])
        mask_sb = sb("mask_sb", [P, 2, DH, D])
        wT = sb("wT", [P, E, DH, D], fp16)

        before = prod[:, :, :, :].rearrange("p a h l -> p (a h l)")
        low = before[0:R, 0:T]
        bc_rest = before[0:96, T:T + L]
        w_nat = before[:, T + L:T + L + DH * D].rearrange("p (h i) -> p h i", h=DH)
        w_neg = before[:, T + L + DH * D:T + L + 2 * DH * D].rearrange("p (h i) -> p h i", h=DH)
        hflat = h[:, :, :, :].rearrange("p a h l -> p (a h l)")
        wx_nat = hflat[0:96, 0:D]
        rw_nat = hflat[0:E, D:2 * D]
        wd_nat = hflat[:, 2 * D:2 * D + DH * R].rearrange("p (h r) -> p h r", h=DH)
        bc_mid = hflat[0:96, 1024:1024 + L // 2].bitcast(bf16)
        xs_sb = hflat[:, 0:4 * D].bitcast(fp16).rearrange("p (j c) -> p j c", j=4)
        xsT = hflat[:, 1024:1024 + 4 * P].bitcast(fp16).rearrange("p (j q t) -> p j q t", j=2, q=4)
        ys_sb = hflat[:, 2048:2048 + 2 * D].rearrange("p (j d) -> p j d", j=2)
        after = dA[:, :, :, :].rearrange("p a h l -> p (a h l)")
        diff, ex, cand, where, over = (after[:, n * TB * E:(n + 1) * TB * E].rearrange("p (a b) -> p a b", a=a)
                                       for n, a in enumerate([TB, TB, TB, TB, E]))
        past = after[:, 5 * TB * E:5 * TB * E + SLOT_TILES * E].rearrange("p (s e) -> p s e", e=E)
        hl = delta[:, :, :].bitcast(fp16).rearrange("p h (t c) -> p (h t) c", c=2 * D)
        xn2T = u
        ytok = xnT[:, :, :].rearrange("p h (t c) -> p (h t) c", c=D)
        res = yT[:, :, :].rearrange("p h (t c) -> p (h t) c", c=D)
        mx = sb("mx", [P, TB])
        se = sb("se", [P, TB])
        top_w = sb("top_w", [P, TB])
        first = sb("first", [P, TB])
        oh = sb("oh", [P, TB, E], bf16)
        cnt = sb("cnt", [P, E])
        ntile = sb("ntile", [P, E])
        incl = sb("incl", [P, E])
        base = sb("base", [P, E])
        pos_f = sb("pos_f", [P, TB])
        pos = sb("pos", [P, TB], i32)
        te_f = sb("te_f", [P, SLOT_TILES])
        te = sb("te", [P, SLOT_TILES], i32)
        zero = sb("zero", [P, 2 * D], fp16)

        bank = ctx.enter_context(nc.psum_tensor("bank", [P, 8, HC], fp32))
        yacc = bank[:, 0:4, :].rearrange("p (h c) n -> p h (c n)", h=DH)
        b_ps = bank[:, 4:6, :].rearrange("p c n -> p (c n)")
        c_ps = bank[:, 6, :]
        w_ps = bank[:, 7, :]

        s_x = [sem(f"x_loaded{b}") for b in range(B)]
        s_small = sem("small_loaded")
        s_mask = [sem(f"mask_loaded{j}") for j in range(2)]
        s_zeroed = sem("sorted_zeroed")
        s_cast = sem("constants_cast")
        s_zero = sem("zeros_ready")
        s_wq = sem("ternary_ready")
        s_wps = sem("weights_transposed")
        s_wsb = sem("weights_evacuated")
        s_amul = sem("a_exp_ready")
        s_a = sem("a_ready")
        s_ve = sem("variance_ready")
        s_r0 = sem("rstd_guess")
        s_xn = sem("xn_ready")
        s_xnps = sem("xn_transposed")
        s_xnsb = sem("xnT_ready")
        s_xd = sem("projected")
        s_low = sem("low_ready")
        s_bchi = sem("bc_read")
        s_bcr = sem("bc_rest_ready")
        s_bcs = sem("bc_step")
        s_bc3 = sem("bc3_ready")
        s_z = sem("z_ready")
        s_act = sem("act_step")
        s_abs = sem("abs_ready")
        s_soft = sem("log1p_ready")
        s_relu = sem("relu_ready")
        s_delta = sem("delta_ready")
        s_u = sem("u_ready")
        s_diag = sem("diag_ready")
        s_dve = sem("dve_step")
        s_bready = sem("b_ready")
        s_bused = sem("b_used")
        s_cready = sem("c_ready")
        s_cevac = sem("c_evacuated")
        s_da = sem("decay_ready")
        s_bx = sem("bx_ready")
        s_scan = sem("scan_done")
        s_prod = sem("product_ready")
        s_sum = sem("product_summed")
        s_mps = sem("mask_transposed")
        s_wt = sem("expert_weight_ready")
        s_yT = sem("yT_ready")
        s_yps = sem("y_transposed")
        s_x1 = sem("x1_ready")
        s_hi = sem("high_ready")
        s_lo = sem("low_part_ready")
        s_x2ps = sem("xn2_transposed")
        s_x2T = sem("xn2T_ready")
        s_logit = sem("logits_ready")
        s_diff = sem("diff_ready")
        s_ex = sem("exp_ready")
        s_oh = sem("onehot_ready")
        s_rank = sem("ranks_ready")
        s_pos = sem("positions_ready")
        s_te = sem("tile_experts_ready")
        s_scat = sem("scattered")
        s_xs = [sem(f"tile_loaded{j}") for j in range(4)]
        s_tps = sem("tile_transposed")
        s_tsb = sem("tile_evacuated")
        s_mm = sem("tile_multiplied")
        s_ysb = sem("tile_scaled")
        s_ys = [sem(f"tile_stored{j}") for j in range(2)]
        s_gath = [sem(f"gathered{q}") for q in range(2)]
        s_res = sem("result_ready")
        s_out = sem("result_stored")

        x_v = x.rearrange("b (t p) d -> p b t d", p=P)
        out_v = out.rearrange("b (t p) d -> p b t d", p=P)
        N_SMALL = 9

        block = ctx.enter_context(nc.Block())

        @block.sync
        def _(sp):
            sp.dma_start(x_sb[:, 0:LB, :], x_v[:, 0, :, :]).then_inc(s_x[0], 16)
            sp.dma_start(cst[:, :], consts).then_inc(s_small, 16)
            sp.dma_start(wx_nat[:, :], w_xproj).then_inc(s_small, 16)
            sp.dma_start(wd_nat[:, :, :], w_dt.rearrange("(h p) r -> p h r", p=P)).then_inc(s_small, 16)
            sp.dma_start(bdt[:, :], b_dt.rearrange("(h p) -> p h", p=P),
                         allow_slow_non_contiguous=True).then_inc(s_small, 16)
            sp.dma_start(dsk[:, :], d_skip.rearrange("(h p) -> p h", p=P),
                         allow_slow_non_contiguous=True).then_inc(s_small, 16)
            sp.dma_start(alog[:, :, :], a_log.rearrange("(h p) n -> p h n", p=P)).then_inc(s_small, 16)
            sp.dma_start(x_sb[:, LB:TB, :], x_v[:, 1, :, :]).then_inc(s_x[1], 16)
            sp.dma_start(w_nat[:, :, :], weight.rearrange("(h p) i -> p h i", p=P)).then_inc(s_small, 16)
            sp.dma_start(rw_nat[:, :], router_w).then_inc(s_small, 16)
            sp.dma_start(scale_bc[:, :], scale.partition_broadcast(P)).then_inc(s_small, 16)

            def load_mask(e, j):
                sp.dma_start(mask_sb[:, j, :, :], masks[bass.ds(e, 1), :, :].rearrange("e (h p) i -> p (e h) i", p=P)
                             ).then_inc(s_mask[j], 16)

            for j in range(2):
                load_mask(j, j)
            sp.wait_ge(s_zero, 1)
            sp.dma_start(xs.rearrange("(t p) c -> p t c", p=P),
                         zero[:, :].unsqueeze(1).to_broadcast([P, SLOT_TILES, 2 * D])).then_inc(s_zeroed, 16)
            with sp.Fori(1, E // 2) as i:
                for j in range(2):
                    sp.wait_ge(s_mps, i * 2 + (j - 1))
                    load_mask(i * 2 + j, j)
            sp.wait_ge(s_scat, 16 * TB)
            def load_tile(t, j):
                sp.dma_start(xs_sb[:, j, :], xs[bass.ds(t * P, P), :]).then_inc(s_xs[j], 16)
            for j in range(4):
                load_tile(j, j)
            with sp.Fori(1, SLOT_TILES // 4) as i:
                for j in range(4):
                    sp.wait_ge(s_tps, i * 4 + (j - 3))
                    load_tile(i * 4 + j, j)
            for t in range(TB):
                sp.wait_ge(s_res, t + 1)
                sp.dma_start(out_v[:, t // LB, t % LB, :], res[:, t, :]).then_inc(s_out, 16)
            sp.wait_ge(s_out, 16 * TB)

        @block.gpsimd
        def _(pool):
            pool.memset(zero[:, :], 0.0).then_inc(s_zero, 1)
            for b in range(B):
                rows = slice(b * L, (b + 1) * L)
                pool.wait_ge(s_bcr, b + 1)
                pool.tensor_copy(bc_mid[:, :], bc_rest[:, :]).then_inc(s_bcs, 1)
                pool.wait_ge(s_bcs, 2 * b + 1)
                pool.tensor_tensor(bc3[64:96, rows], bc_rest[64:96, :], bc_mid[64:96, :], ALU.subtract).then_inc(s_bcs, 1)
                pool.wait_ge(s_bcs, 2 * b + 2)
                pool.tensor_copy(bc3[32:64, rows], bc_mid[32:64, :]).then_inc(s_bc3, 1)

            def products(k, j, head=False):
                pool.wait_ge(s_cevac, k * 2 + 2)
                for dh in range(DH):
                    pool.wait_ge(s_scan, k * 2 + (dh + 1))
                    if not head:
                        pool.wait_ge(s_sum, k * 2 + (dh - 3))
                    pool.tensor_tensor(prod[:, j, dh, :], h[:, j, dh, :], cb[:, j, :], ALU.mult).then_inc(s_prod, 1)

            for j in range(2):
                products(j, j, head=True)
            with pool.Fori(1, B * N // 2) as i:
                for j in range(2):
                    products(i * 2 + j, j)

            pool.wait_ge(s_zeroed, 16)
            pool.wait_ge(s_pos, 1)
            for t in range(TB):
                pool.indirect_dma_start(xs, bass.IndirectOffsetOnAxis(ap=pos[:, t:t + 1], axis=0),
                                        hl[:, t, :], None).then_inc(s_scat, 16)
            for j in range(2):
                pool.wait_ge(s_ys[j], 16 * (SLOT_TILES // 2))
            for t in range(TB):
                pool.indirect_dma_start(ytok[:, t, :], None, ys,
                                        bass.IndirectOffsetOnAxis(ap=pos[:, t:t + 1], axis=0)).then_inc(s_gath[t // LB], 16)

        @block.scalar
        def _(act):
            act.wait_ge(s_small, 16 * (N_SMALL))
            act.activation(ident16[:, :], ident, ACT.Copy).then_inc(s_cast, 1)
            act.activation(tri_bf[:, :], cst[:, C_TRI:C_TRI + P], ACT.Copy).then_inc(s_cast, 1)
            act.activation(ones_bf[:, :], cst[:, C_ONE:C_ONE + P], ACT.Copy).then_inc(s_cast, 1)
            act.activation(a_exp[:, :, :], alog[:, :, :], ACT.Exp).then_inc(s_amul, 1)
            act.wait_ge(s_wps, 1)
            wx_ps = bank[:, 4, 0:DH * 96].rearrange("p (h k) -> p h k", h=DH)
            act.activation(wxT[:, :, 0:R], wx_ps[:, :, 0:R], ACT.Copy).then_inc(s_wsb, 1)
            for g in range(3):
                act.activation(wxT[:, :, R + 32 * g:R + 32 * g + 32], wx_ps[:, :, R:96], ACT.Copy).then_inc(s_wsb, 1)
            act.wait_ge(s_wps, 2)
            act.activation(wdT[:, :], bank[0:R, 5, 0:D], ACT.Copy).then_inc(s_wsb, 1)
            act.wait_ge(s_wps, 3)
            act.activation(rwT[:, :, :], bank[:, 6, 0:DH * E].rearrange("p (h e) -> p h e", h=DH), ACT.Copy).then_inc(s_wsb, 1)
            act.wait_ge(s_wps, 4)
            act.activation(wqT[:, :, :], bank[:, 7, :].rearrange("p (h o) -> p h o", h=DH), ACT.Copy).then_inc(s_wsb, 1)

            def rstd_guess(n, blocks):
                act.wait_ge(s_ve, n)
                act.activation(lnv[:, blocks], ve[:, blocks], ACT.Ln).then_inc(s_act, 1)
                act.wait_ge(s_act, steps.pop(0))
                act.activation(r0[:, blocks], lnv[:, blocks], ACT.Exp, scale=-0.5).then_inc(s_r0, 1)

            steps = list(range(1, 100))
            for b in range(B):
                rstd_guess(b + 1, slice(b * LB, (b + 1) * LB))
            for b in range(B):
                for q in range(DH * LH):
                    act.wait_ge(s_xnps, DH * LH * b + q + 1)
                    dh, c = q // LH, q % LH
                    act.activation(xnT[:, dh, b * L + c * HC:b * L + (c + 1) * HC], bank[:, q, :], ACT.Copy).then_inc(s_xnsb, 1)
                for c in range(LH):
                    act.wait_ge(s_xd, LH * b + c + 1)
                    act.activation(low[:, b * L + c * HC:b * L + (c + 1) * HC], bank[0:R, 4 + c, :], ACT.Copy).then_inc(s_low, 1)
                for dh in range(DH):
                    act.wait_ge(s_z, DH * b + dh + 1)
                    soft = dA[:, 0, dh, :]
                    if b:
                        act.wait_ge(s_delta, dh + 1)
                    act.activation(soft, yacc[:, dh, :], ACT.Abs, bias=bdt[:, dh:dh + 1]).then_inc(s_abs, 1)
                    act.wait_ge(s_abs, DH * b + dh + 1)
                    act.activation(soft, soft, ACT.Exp, scale=-1.0).then_inc(s_act, 1)
                    act.wait_ge(s_act, steps.pop(0))
                    act.activation(soft, soft, ACT.Ln, bias=1.0).then_inc(s_soft, 1)

            act.wait_ge(s_a, 1)
            act.wait_ge(s_delta, B * DH)

            def c_rows(k, j, head=False):
                if not head:
                    act.wait_ge(s_prod, k * 2 - 2)
                for c in range(LH):
                    act.wait_ge(s_cready, k * 2 + (c + 1))
                    act.activation(cb[:, j, c * HC:(c + 1) * HC], c_ps, ACT.Copy).then_inc(s_cevac, 1)

            def decays(b, n, k, j, head=False):
                for dh in range(DH):
                    if not head:
                        act.wait_ge(s_scan, k * 2 + (dh - 3))
                    act.activation(dA[:, j, dh, :], delta[:, dh, b * L:(b + 1) * L], ACT.Exp,
                                   scale=a_neg[:, dh, bass.ds(n, 1)]).then_inc(s_da, 1)

            def y_out(b):
                act.wait_ge(s_sum, DH * N * (b + 1))
                for dh in range(DH):
                    act.activation(yT[:, dh, b * L:(b + 1) * L], yacc[:, dh, :], ACT.Copy).then_inc(s_yT, 1)

            for b in range(B):
                for j in range(2):
                    decays(b, j, b * N + j, j, head=(b == 0))
                    c_rows(b * N + j, j, head=(b == 0))
                    if b and j == 0:
                        y_out(b - 1)
                with act.Fori(1, N // 2) as i:
                    for j in range(2):
                        n = i * 2 + j
                        decays(b, n, n + b * N, j)
                        c_rows(n + b * N, j)
            y_out(B - 1)

            rstd_guess(B + 1, slice(0, TB))
            for q in range(2 * B * DH):
                act.wait_ge(s_x2ps, q + 1)
                dh, c = q // 4, q % 4
                act.activation(xn2T[:, dh, c * HC:(c + 1) * HC], bank[:, q, :], ACT.Copy).then_inc(s_x2T, 1)
            act.wait_ge(s_diff, 1)
            act.activation(ex[:, :, :], diff[:, :, :], ACT.Exp).then_inc(s_ex, 1)
            def turned(t, j, head=False):
                act.wait_ge(s_tps, t + 1)
                if not head:
                    act.wait_ge(s_mm, t - 1)
                act.activation(xsT[:, j, :, :], bank[:, j, 0:2 * P].bitcast(fp16).rearrange("p (q t) -> p q t", q=4),
                               ACT.Copy).then_inc(s_tsb, 1)

            def store(t, j):
                act.wait_ge(s_ysb, t + 1)
                act.dma_start(ys[bass.ds(t * P, P), :], ys_sb[:, j, :]).then_inc(s_ys[j], 16)

            turned(0, 0, head=True)
            turned(1, 1, head=True)
            with act.Fori(1, SLOT_TILES // 2) as i:
                for j in range(2):
                    turned(i * 2 + j, j)
                    store(i * 2 + (j - 2), j)
            for t in range(SLOT_TILES - 2, SLOT_TILES):
                store(t, t % 2)

        @block.vector
        def _(dve):
            step = [0]

            def then_next(ins):
                step[0] += 1
                ins.then_inc(s_dve, 1)
                dve.wait_ge(s_dve, step[0])

            def norm_stats(blocks):
                for t in range(blocks.start, blocks.stop):
                    last = dve.bn_stats(st[:, t, :], x_sb[:, t, :])
                then_next(last)
                for t in range(blocks.start, blocks.stop):
                    last = dve.bn_aggr(mv[:, t, :], st[:, t, :])
                then_next(last)
                dve.tensor_scalar(ve[:, blocks], mv[:, blocks, 1], EPS, None, ALU.add).then_inc(s_ve, 1)

            def norm_apply(n, blocks, done):
                dve.wait_ge(s_r0, n)
                then_next(dve.tensor_tensor(rr[:, blocks], r0[:, blocks], r0[:, blocks], ALU.mult))
                then_next(dve.tensor_tensor(rt[:, blocks], rr[:, blocks], ve[:, blocks], ALU.mult))
                then_next(dve.tensor_scalar(rr[:, blocks], rt[:, blocks], -0.5, 1.5, ALU.mult, ALU.add))
                then_next(dve.tensor_tensor(rstd[:, blocks], rr[:, blocks], r0[:, blocks], ALU.mult))
                for t in range(blocks.start, blocks.stop):
                    dve.tensor_scalar(xn[:, t, :], x_sb[:, t, :], mv[:, t, 0:1], rstd[:, t:t + 1],
                                      ALU.subtract, ALU.mult).then_inc(done, 1)

            halves = [slice(b * LB, (b + 1) * LB) for b in range(B)]
            dve.wait_ge(s_x[0], 16)
            norm_stats(halves[0])
            dve.wait_ge(s_small, 16 * N_SMALL)
            then_next(dve.tensor_scalar(w_neg[:, :, :], w_nat[:, :, :], -0.25, None, ALU.is_lt))
            dve.scalar_tensor_tensor(w_nat[:, :, :], w_nat[:, :, :], 0.25, w_neg[:, :, :], ALU.is_gt, ALU.subtract).then_inc(s_wq, 1)
            norm_apply(1, halves[0], s_xn)
            dve.wait_ge(s_x[1], 16)
            norm_stats(halves[1])
            dve.wait_ge(s_amul, 1)
            dve.tensor_scalar(a_neg[:, :, :], a_exp[:, :, :], -1.0, None, ALU.mult).then_inc(s_a, 1)
            then_next(dve.tensor_tensor(pick[:, :], ident[0:96, 0:32], ident[0:96, 32:64], ALU.add))
            dve.tensor_tensor(pick[:, :], pick[:, :], ident[0:96, 64:96], ALU.add).then_inc(s_diag, 1)
            for dh in range(DH):
                dve.tensor_scalar(diag_d[:, dh, :], ident, dsk[:, dh:dh + 1], None, ALU.mult).then_inc(s_diag, 1)
            norm_apply(2, halves[1], s_xn)

            for b in range(B):
                rows = slice(b * L, (b + 1) * L)
                bc_ps = bank[0:96, 6:8, :].rearrange("p c n -> p (c n)")
                dve.wait_ge(s_xd, LH * (b + 1))
                if b:
                    dve.wait_ge(s_bc3, b)
                then_next(dve.tensor_copy(bc3[:, rows], bc_ps))
                dve.tensor_tensor(bc_rest[:, :], bc_ps, bc3[:, rows], ALU.subtract).then_inc(s_bcr, 1)
                for dh in range(DH):
                    dve.wait_ge(s_abs, DH * b + dh + 1)
                    dve.tensor_scalar(delta[:, dh, rows], yacc[:, dh, :], bdt[:, dh:dh + 1], 0.0,
                                      ALU.add, ALU.max).then_inc(s_relu, 1)
                for dh in range(DH):
                    dve.wait_ge(s_soft, DH * b + dh + 1)
                    dve.wait_ge(s_relu, DH * b + dh + 1)
                    dve.tensor_tensor(delta[:, dh, rows], delta[:, dh, rows], dA[:, 0, dh, :], ALU.add).then_inc(s_delta, 1)
                for dh in range(DH):
                    dve.wait_ge(s_delta, DH * b + dh + 1)
                    dve.tensor_tensor(u[:, dh, rows], delta[:, dh, rows], xnT[:, dh, rows], ALU.mult).then_inc(s_u, 1)

            dve.wait_ge(s_u, B * DH)
            dve.wait_ge(s_wsb, 7)

            def scans(b, k, j, head=False):
                rows = slice(b * L, (b + 1) * L)
                dve.wait_ge(s_bready, k + 1)
                for dh in range(DH):
                    if not (head and j == 0):
                        dve.wait_ge(s_scan, k * 2 + (dh - 1))
                    dve.tensor_tensor(bx[:, dh, :], b_ps, u[:, dh, rows], ALU.mult).then_inc(s_bx, 1)
                for dh in range(DH):
                    dve.wait_ge(s_bx, k * 2 + (dh + 1))
                    dve.wait_ge(s_da, k * 2 + (dh + 1))
                    if not head:
                        dve.wait_ge(s_prod, k * 2 + (dh - 3))
                    dve.tensor_tensor_scan(h[:, j, dh, :], dA[:, j, dh, :], bx[:, dh, :], 0.0,
                                           ALU.mult, ALU.add).then_inc(s_scan, 1)
                dve.wait_ge(s_mps, k + 1)
                dve.tensor_tensor(wT[:, bass.ds(k, 1), :, :].rearrange("p e h o -> p (e h o)"), w_ps,
                                  wqT[:, :, :].rearrange("p h o -> p (h o)"), ALU.mult).then_inc(s_wt, 1)

            for b in range(B):
                if b == 0:
                    for j in range(2):
                        scans(b, j, j, head=True)
                with dve.Fori(1 if b == 0 else 0, N // 2) as i:
                    for j in range(2):
                        scans(b, i * 2 + (j + b * N), j)

            for g in range(8):
                dve.wait_ge(s_yps, g + 1)
                dve.tensor_tensor(x_sb[:, 2 * g:2 * g + 2, :].rearrange("p t d -> p (t d)"), bank[:, g, :],
                                  x_sb[:, 2 * g:2 * g + 2, :].rearrange("p t d -> p (t d)"), ALU.add).then_inc(s_x1, 1)
            dve.wait_ge(s_x1, 8)
            norm_stats(slice(0, TB))
            norm_apply(B + 1, slice(0, TB), s_hi)
            dve.wait_ge(s_hi, TB)
            for t in range(TB):
                last = dve.tensor_copy(hl[:, t, 0:D], xn[:, t, :])
            then_next(last)
            for t in range(TB):
                dve.tensor_tensor(hl[:, t, D:2 * D], xn[:, t, :], hl[:, t, 0:D], ALU.subtract).then_inc(s_lo, 1)
            logits = bank[:, 0, :].rearrange("p (t e) -> p t e", e=E)
            dve.wait_ge(s_logit, 1)
            then_next(dve.tensor_reduce(mx[:, :], logits, AX.X, ALU.max))
            dve.tensor_tensor(diff[:, :, :], logits, mx[:, :].unsqueeze(2).to_broadcast([P, TB, E]), ALU.subtract).then_inc(s_diff, 1)
            dve.wait_ge(s_diff, 1)
            from_end = cst[:, C_RE:C_RE + E].unsqueeze(1).to_broadcast([P, TB, E])
            then_next(dve.scalar_tensor_tensor(cand[:, :, :], diff[:, :, :], 0.0, from_end, ALU.is_equal, ALU.mult))
            then_next(dve.tensor_reduce(first[:, :], cand[:, :, :], AX.X, ALU.max))
            dve.tensor_tensor(oh[:, :, :], from_end, first[:, :].unsqueeze(2).to_broadcast([P, TB, E]), ALU.is_equal).then_inc(s_oh, 1)
            dve.wait_ge(s_ex, 1)
            then_next(dve.tensor_reduce(se[:, :], ex[:, :, :], AX.X, ALU.add))
            then_next(dve.reciprocal(top_w[:, :], se[:, :]))
            dve.wait_ge(s_rank, 1)
            then_next(dve.tensor_copy(cnt[:, :], bank[:, 2, 0:E]))
            then_next(dve.tensor_tensor(over[:, :, :], cnt[:, :].unsqueeze(2).to_broadcast([P, E, TB]),
                                        cst[:, C_CNT:C_CNT + TB].unsqueeze(1).to_broadcast([P, E, TB]), ALU.is_gt))
            then_next(dve.tensor_reduce(ntile[:, :], over[:, :, :], AX.X, ALU.add))
            then_next(dve.tensor_tensor_scan(incl[:, :], cst[:, C_ONE:C_ONE + E], ntile[:, :], 0.0, ALU.mult, ALU.add))
            then_next(dve.tensor_tensor(base[:, :], incl[:, :], ntile[:, :], ALU.subtract))
            then_next(dve.scalar_tensor_tensor(where[:, :, :], base[:, :].unsqueeze(1).to_broadcast([P, TB, E]), float(P),
                                               bank[:, 1, :].rearrange("p (t e) -> p t e", e=E), ALU.mult, ALU.add))
            then_next(dve.tensor_tensor(where[:, :, :], where[:, :, :], oh[:, :, :], ALU.mult))
            then_next(dve.tensor_reduce(pos_f[:, :], where[:, :, :], AX.X, ALU.add))
            dve.wait_ge(s_lo, TB)
            dve.tensor_copy(pos[:, :], pos_f[:, :]).then_inc(s_pos, 1)
            then_next(dve.tensor_tensor(past[:, :, :], incl[:, :].unsqueeze(1).to_broadcast([P, SLOT_TILES, E]),
                                        cst[:, C_TILE:C_TILE + SLOT_TILES].unsqueeze(2).to_broadcast([P, SLOT_TILES, E]), ALU.is_le))
            then_next(dve.tensor_reduce(te_f[:, :], past[:, :, :], AX.X, ALU.add))
            dve.tensor_scalar(te[:, :], te_f[:, :], float(E - 1), None, ALU.min).then_inc(s_te, 1)

            def scaled(t, j, head=False):
                dve.wait_ge(s_mm, t + 1)
                if not head:
                    dve.wait_ge(s_ys[j], (t // 2) * 16 if isinstance(t, int) else None)
                dve.tensor_tensor(ys_sb[:, j, :], bank[:, 4 + j, 0:D], scale_bc[:, :], ALU.mult).then_inc(s_ysb, 1)

            for j in range(2):
                scaled(j, j, head=True)
            with dve.Fori(1, SLOT_TILES // 2) as i:
                for j in range(2):
                    dve.wait_ge(s_mm, i * 2 + (j + 1))
                    dve.wait_ge(s_ys[j], i * 16)
                    dve.tensor_tensor(ys_sb[:, j, :], bank[:, 4 + j, 0:D], scale_bc[:, :], ALU.mult).then_inc(s_ysb, 1)
            for t in range(TB):
                if t % LB == 0:
                    dve.wait_ge(s_gath[t // LB], 16 * LB)
                dve.scalar_tensor_tensor(res[:, t, :], ytok[:, t, :], top_w[:, t:t + 1], x_sb[:, t, :],
                                         ALU.mult, ALU.add).then_inc(s_res, 1)

        @block.tensor
        def _(pe):
            pe.wait_ge(s_small, 16 * N_SMALL)
            for dh in range(DH):
                mm = pe.transpose(bank[:, 4, 96 * dh:96 * dh + 96], wx_nat[:, dh * P:(dh + 1) * P], ident[0:96, 0:96])
            mm.then_inc(s_wps, 1)
            for dh in range(DH):
                mm = pe.transpose(bank[0:R, 5, dh * P:(dh + 1) * P], wd_nat[:, dh, :], ident)
            mm.then_inc(s_wps, 1)
            for dh in range(DH):
                mm = pe.transpose(bank[:, 6, E * dh:E * dh + E], rw_nat[:, dh * P:(dh + 1) * P], ident[0:E, 0:E])
            mm.then_inc(s_wps, 1)
            pe.wait_ge(s_wq, 1)
            for ic in range(DH):
                for oc in range(DH):
                    mm = pe.transpose(bank[:, 7, ic * D + oc * P:ic * D + (oc + 1) * P],
                                      w_nat[:, oc, ic * P:(ic + 1) * P], ident)
            mm.then_inc(s_wps, 1)

            for b in range(B):
                if b:
                    pe.wait_ge(s_soft, DH * b)
                    pe.wait_ge(s_relu, DH * b)
                for q in range(DH * LH):
                    dh, c = q // LH, q % LH
                    for t in range(4):
                        blk = b * LB + 4 * c + t
                        pe.wait_ge(s_xn, blk + 1)
                        mm = pe.transpose(bank[:, q, t * P:(t + 1) * P], xn[:, blk, dh * P:(dh + 1) * P], ident)
                    mm.then_inc(s_xnps, 1)
                pe.wait_ge(s_xnsb, DH * LH * (b + 1))
                if b == 0:
                    pe.wait_ge(s_wsb, 7)
                else:
                    pe.wait_ge(s_low, LH * b)
                    pe.wait_ge(s_bcr, b)
                for c in range(LH):
                    cols = slice(b * L + c * HC, b * L + (c + 1) * HC)
                    for dh in range(DH):
                        pe.matmul(bank[0:R, 4 + c, :], wxT[:, dh, 0:R], xnT[:, dh, cols], start=(dh == 0), stop=(dh == DH - 1))
                    for dh in range(DH):
                        mm = pe.matmul(bank[0:96, 6 + c, :], wxT[:, dh, R:R + 96], xnT[:, dh, cols],
                                       start=(dh == 0), stop=(dh == DH - 1))
                    mm.then_inc(s_xd, 1)
                pe.wait_ge(s_low, LH * (b + 1))
                for dh in range(DH):
                    for c in range(LH):
                        cols = slice(b * L + c * HC, b * L + (c + 1) * HC)
                        mm = pe.matmul(bank[:, LH * dh + c, :], wdT[:, dh * P:(dh + 1) * P], low[:, cols], start=True, stop=True)
                    mm.then_inc(s_z, 1)

            pe.wait_ge(s_bc3, B)
            pe.wait_ge(s_diag, 1 + DH)
            pe.wait_ge(s_delta, B * DH)
            pe.wait_ge(s_bcr, B)
            pe.wait_ge(s_low, B * LH)

            def rows_out(b, n, k, head=False):
                if not head:
                    pe.wait_ge(s_bx, k * 2)
                pick_b = pick[:, bass.ds(n, 1)].to_broadcast([96, P])
                pick_c = pick[:, bass.ds(n + N, 1)].to_broadcast([96, P])
                for c in range(LH):
                    cols = slice(b * L + c * HC, b * L + (c + 1) * HC)
                    mm = pe.matmul(b_ps[:, c * HC:(c + 1) * HC], pick_b, bc3[:, cols], start=True, stop=True)
                mm.then_inc(s_bready, 1)
                for c in range(LH):
                    cols = slice(b * L + c * HC, b * L + (c + 1) * HC)
                    if not (head and c == 0):
                        pe.wait_ge(s_cevac, k * 2 + c)
                    pe.matmul(c_ps, pick_c, bc3[:, cols], start=True, stop=True).then_inc(s_cready, 1)

            def masks_turned(k, j, times, head=False):
                pe.wait_ge(s_mask[j], times)
                if not head:
                    pe.wait_ge(s_wt, k)
                for ic in range(DH):
                    for oc in range(DH):
                        mm = pe.transpose(w_ps[:, ic * D + oc * P:ic * D + (oc + 1) * P],
                                          mask_sb[:, j, oc, ic * P:(ic + 1) * P], ident)
                mm.then_inc(s_mps, 1)

            def skip_term(b):
                for dh in range(DH):
                    for c in range(LH):
                        cols = slice(b * L + c * HC, b * L + (c + 1) * HC)
                        pe.matmul(yacc[:, dh, c * HC:(c + 1) * HC], diag_d[:, dh, :], xnT[:, dh, cols],
                                  start=True, stop=False, skip_group_check=True)

            def sums(k, j, last=False):
                for dh in range(DH):
                    pe.wait_ge(s_prod, k * 2 + (dh + 1))
                    for c in range(LH):
                        mm = pe.matmul(yacc[:, dh, c * HC:(c + 1) * HC], ident, prod[:, j, dh, c * HC:(c + 1) * HC],
                                       start=False, stop=last, skip_group_check=True)
                    mm.then_inc(s_sum, 1)
                return mm

            for b in range(B):
                if b == 0:
                    skip_term(b)
                    rows_out(b, 0, 0, head=True)
                    masks_turned(0, 0, 16, head=True)
                    rows_out(b, 1, 1)
                    masks_turned(1, 1, 16)
                    sums(0, 0)
                else:
                    rows_out(b, 0, b * N)
                    masks_turned(b * N, 0, (b * N // 2 + 1) * 16)
                    sums(b * N - 1, 1, last=True)
                    pe.wait_ge(s_yT, DH * b)
                    skip_term(b)
                    rows_out(b, 1, b * N + 1)
                    masks_turned(b * N + 1, 1, (b * N // 2 + 1) * 16)
                    sums(b * N, 0)
                with pe.Fori(1, N // 2) as i:
                    for j in range(2):
                        n = i * 2 + j
                        k = i * 2 + (j + b * N)
                        rows_out(b, n, k)
                        masks_turned(k, j, i * 16 + 16 * (1 + b * N // 2))
                        sums(k - 1, 1 - j)
            sums(B * N - 1, 1, last=True)

            pe.wait_ge(s_yT, DH * B)
            pe.wait_ge(s_bx, B * N * DH)
            pe.wait_ge(s_cevac, B * N * LH)
            pe.wait_ge(s_wt, E)
            for g in range(8):
                for t in range(2):
                    for dh in range(DH):
                        blk = 2 * g + t
                        mm = pe.transpose(bank[:, g, t * D + dh * P:t * D + (dh + 1) * P],
                                          yT[:, dh, blk * P:(blk + 1) * P], ident)
                mm.then_inc(s_yps, 1)
            pe.wait_ge(s_x1, 8)
            for q in range(8):
                dh, c = q // 4, q % 4
                for t in range(4):
                    blk = 4 * c + t
                    pe.wait_ge(s_hi, blk + 1)
                    mm = pe.transpose(bank[:, q, t * P:(t + 1) * P], xn[:, blk, dh * P:(dh + 1) * P], ident)
                mm.then_inc(s_x2ps, 1)
            pe.wait_ge(s_x2T, 8)
            for t in range(TB):
                for dh in range(DH):
                    mm = pe.matmul(bank[:, 0, t * E:(t + 1) * E], xn2T[:, dh, t * P:(t + 1) * P], rwT[:, dh, :],
                                   start=(dh == 0), stop=(dh == DH - 1))
            mm.then_inc(s_logit, 1)
            pe.wait_ge(s_oh, 1)
            pe.wait_ge(s_cast, 3)
            oh_f = oh[:, :, :].rearrange("p t e -> p (t e)")
            pe.matmul(bank[:, 1, :], tri_bf[:, :], oh_f, start=True, stop=False, skip_group_check=True)
            for s in range(1, TB):
                mm = pe.matmul(bank[:, 1, s * E:], ones_bf[:, :], oh_f[:, 0:(TB - s) * E], start=False,
                               stop=(s == TB - 1), skip_group_check=True)
            for t in range(TB):
                mm = pe.matmul(bank[:, 2, 0:E], ones_bf[:, :], oh[:, t, :], start=(t == 0), stop=(t == TB - 1))
            mm.then_inc(s_rank, 1)

            pe.wait_ge(s_te, 1)

            def turn(t, j4, times, head=False):
                j = j4 % 2
                pe.wait_ge(s_xs[j4], times)
                if not head:
                    pe.wait_ge(s_tsb, t - 1)
                tps = bank[:, j, 0:2 * P].bitcast(fp16)
                for q in range(4):
                    mm = pe.transpose(tps[:, q * P:(q + 1) * P], xs_sb[:, j4, q * P:(q + 1) * P], ident16[:, :])
                mm.then_inc(s_tps, 1)

            def multiply(t, j, head=False):
                expert = pe.value_load(te[0:1, bass.ds(t, 1)], min_val=0, max_val=E - 1)
                pe.wait_ge(s_tsb, t + 1)
                if not head:
                    pe.wait_ge(s_ysb, t - 1)
                for q in range(4):
                    mm = pe.matmul(bank[:, 4 + j, 0:D], xsT[:, j, q, :],
                                   wT[:, bass.ds(expert, 1), q % 2, :].rearrange("p e o -> p (e o)"),
                                   start=(q == 0), stop=(q == 3))
                mm.then_inc(s_mm, 1)

            turn(0, 0, 16, head=True)
            turn(1, 1, 16, head=True)
            multiply(0, 0, head=True)
            turn(2, 2, 16)
            multiply(1, 1, head=True)
            turn(3, 3, 16)
            multiply(2, 0)
            with pe.Fori(1, SLOT_TILES // 4) as i:
                for j in range(4):
                    turn(i * 4 + j, j, i * 16 + 16)
                    multiply(i * 4 + (j - 1), (j - 1) % 2)
            multiply(SLOT_TILES - 1, 1)


_INS = ['L0_attn_x', 'L0_attn_W_xproj', 'L0_attn_W_dt', 'L0_attn_b_dt', 'L0_attn_A_log', 'L0_attn_D',
        'L0_ffn_weight', 'L0_ffn_scale', 'L0_ffn_expert_masks', 'L0_ffn_router_w']


def _constants():
    import numpy as np
    c = np.zeros((P, C_END), np.float32)
    c[:, C_ID:C_ID + P] = np.eye(P)
    c[:, C_TRI:C_TRI + P] = np.triu(np.ones((P, P)), 1)
    c[:, C_ONE:C_ONE + P] = 1.0
    c[:, C_RE:C_RE + E] = E - np.arange(E)
    c[:, C_CNT:C_CNT + TB] = P * np.arange(TB)
    c[:, C_TILE:C_TILE + SLOT_TILES] = np.arange(SLOT_TILES)
    return c


def kernel(**inputs):
    import numpy as _np
    import concourse.bacc as _bacc
    from concourse import mybir as _mybir
    from concourse.bass_utils import run_bass_kernel_spmd as _run

    nc = _bacc.Bacc("TRN2", target_bir_lowering=False, num_devices=1)
    arrays, args = {}, []
    for name in _INS + ["constants"]:
        a = _constants() if name == "constants" else _np.ascontiguousarray(inputs[name])
        arrays[f"in_{name}_dram"] = a
        args.append(nc.dram_tensor(f"in_{name}_dram", a.shape, _mybir.dt.from_np(a.dtype), kind="ExternalInput").ap())
    args.append(nc.dram_tensor("out_0_dram", (B, L, D), _mybir.dt.float32, kind="ExternalOutput").ap())
    selective_scan_then_routed_ternary_ffn(nc, *args)
    r = _run(nc, [arrays], core_ids=[0])
    return r.results[0]["out_0_dram"]
```

```python
import concourse.bass as bass
from concourse import mybir
from contextlib import ExitStack

P = 128
B, L, D = 2, 1024, 256
R, N = 64, 16
E = 32
T = B * L
TB = T // P
LB = L // P
DH = D // P
HC = 512
LH = L // HC
M = 64
TILES = 64
SLOTS = TILES * M
BLOCKS = SLOTS // P
QUADS = TILES // 4
LOADS = QUADS // 2
EPS = 1e-5
C_ID, C_TRI, C_ONE, C_RE, C_TILE, C_END = 0, 128, 256, 384, 416, 480


def selective_scan_then_routed_ternary_ffn(nc, x, w_xproj, w_dt, b_dt, a_log, d_skip,
                                           weight, scale, masks, router_w, consts, out):
    fp32, fp16, bf16 = mybir.dt.float32, mybir.dt.float16, mybir.dt.bfloat16
    i32 = mybir.dt.int32
    ALU, ACT, AX = mybir.AluOpType, mybir.ActivationFunctionType, mybir.AxisListType

    xs = nc.dram_tensor("sorted_tokens", (SLOTS, 2 * D), fp16, kind="Internal").ap()
    ys = nc.dram_tensor("sorted_outputs", (SLOTS, D), fp32, kind="Internal").ap()

    ctx = ExitStack()
    with ctx:
        def sb(name, shape, dt=fp32):
            return ctx.enter_context(nc.sbuf_tensor(name, shape, dt))

        def sem(name):
            return ctx.enter_context(nc.semaphore(name))

        cst = sb("cst", [P, C_END])
        ident = cst[:, C_ID:C_ID + P]
        ident16 = sb("ident16", [P, P], fp16)
        tri_bf = sb("tri_bf", [P, P], bf16)
        ones_bf = sb("ones_bf", [P, P], bf16)
        pick = sb("pick", [96, E], bf16)
        x_sb = sb("x_sb", [P, TB, D])
        xn = sb("xn", [P, TB, D])
        xnT = sb("xnT", [P, DH, T])
        delta = sb("delta", [P, DH, T])
        u = sb("u", [P, DH, T])
        yT = xn[:, :, :].rearrange("p t d -> p (t d)").rearrange("p (b h l) -> p b h l", b=B, h=DH)
        bdt = sb("bdt", [P, DH])
        dsk = sb("dsk", [P, DH])
        xd = sb("xd", [96, L])
        alog = sb("alog", [P, DH, N])
        a_exp = sb("a_exp", [P, DH, N])
        a_neg = sb("a_neg", [P, DH, N])
        scale_bc = sb("scale_bc", [P, D])
        wxT = sb("wxT", [P, DH, 96])
        wdT = sb("wdT", [R, D])
        rwT = sb("rwT", [P, DH, E])
        wqT = sb("wqT", [P, DH, D], fp16)
        diag_d = sb("diag_d", [P, DH, P])
        bc3 = sb("bc3", [96, T], bf16)
        st = sb("st", [P, TB, 6])
        mv = sb("mv", [P, TB, 2])
        ve = sb("ve", [P, TB])
        lnv = sb("lnv", [P, TB])
        r0 = sb("r0", [P, TB])
        rr = sb("rr", [P, TB])
        rt = sb("rt", [P, TB])
        rstd = sb("rstd", [P, TB])
        dA = sb("dA", [P, 2, DH, L])
        bx = sb("bx", [P, DH, L])
        h = sb("h", [P, 2, DH, L])
        prod = sb("prod", [P, 2, DH, L])
        cb = sb("cb", [P, 2, L])
        mask_sb = sb("mask_sb", [P, 4, DH, D])
        wT = sb("wT", [P, E, DH, D], fp16)

        flat = "p a h l -> p (a h l)"
        before = prod[:, :, :, :].rearrange(flat)
        w_nat = before[:, 0:DH * D].rearrange("p (h i) -> p h i", h=DH)
        w_neg = before[:, DH * D:2 * DH * D].rearrange("p (h i) -> p h i", h=DH)
        wx_nat = before[0:96, 1024:1024 + D]
        rw_nat = before[0:E, 1280:1280 + D]
        wd_nat = before[:, 1536:1536 + DH * R].rearrange("p (h r) -> p h r", h=DH)
        early = wT[:, :, :, :].rearrange("p e h o -> p (e h o)").bitcast(fp32)
        zb = early[:, 0:4 * HC].rearrange("p (q c) -> p q c", q=4)
        soft = early[:, 4 * HC:8 * HC].rearrange("p (q c) -> p q c", q=4)
        bc_rest = early[:, 8 * HC:10 * HC].rearrange("p (c n) -> p c n", c=LH)
        bc_mid = early[:, 10 * HC:11 * HC].bitcast(bf16).rearrange("p (c n) -> p c n", c=LH)
        bc_low = early[:, 11 * HC:12 * HC].bitcast(bf16).rearrange("p (c n) -> p c n", c=LH)
        after = dA[:, :, :, :].rearrange(flat)
        diff, ex, cand, where = (after[:, n * TB * E:(n + 1) * TB * E].rearrange("p (t e) -> p t e", t=TB)
                                 for n in range(4))
        past = mask_sb[:, :, :, :].rearrange(flat).rearrange("p (t e) -> p t e", e=E)
        xs_sb = h[:, :, :, :].rearrange(flat).bitcast(fp16).rearrange("p (s t c) -> p s t c", s=4, t=4)
        xsT = bx[:, :, :].bitcast(fp16).rearrange("p h (b q t) -> p h b q t", q=4, t=P)[:, :, 0:2, :, :]
        ys_sb = cb[0:M, :, :].rearrange("p j (t d) -> p j t d", d=D)
        hl = delta[:, :, :].bitcast(fp16).rearrange("p h (t c) -> p (h t) c", c=2 * D)
        xn2T = u
        logitsT = after[0:E, 4 * TB * E:4 * TB * E + T]
        ytok = xnT[:, :, :].rearrange("p h (t c) -> p (h t) c", c=D)
        res = xn
        mx = sb("mx", [P, TB])
        se = sb("se", [P, TB])
        spare = bx[:, 1, L // 2:L]
        top_w = sb("top_w", [P, TB])
        first = sb("first", [P, TB])
        oh = spare[:, 0:TB * E // 2].bitcast(bf16).rearrange("p (t e) -> p t e", t=TB)
        cnt, cnt_t, ntile, incl, base = (spare[:, TB * E // 2 + n * E:TB * E // 2 + (n + 1) * E] for n in range(5))
        cnt, cnt_t = cnt.bitcast(i32), cnt_t.bitcast(i32)
        pos_f = sb("pos_f", [P, TB])
        pos = sb("pos", [P, TB], i32)
        te_f = bx[:, 0, L // 2:L // 2 + TILES]
        te = sb("te", [P, TILES], i32)
        zero = sb("zero", [P, 2 * D], fp16)

        bank = ctx.enter_context(nc.psum_tensor("bank", [P, 8, HC], fp32))
        yacc = bank[:, 0:4, :].rearrange("p (h c) n -> p h (c n)", h=DH)
        b_ps = bank[:, 4:6, :].rearrange("p c n -> p (c n)")
        c_ps = bank[:, 6, :]
        w_ps = bank[:, 7, :]

        s_x = [sem(f"x_loaded{q}") for q in range(4)]
        s_cst = sem("constants_loaded")
        s_early = sem("early_weights_loaded")
        s_alog = sem("a_log_loaded")
        s_late = sem("late_weights_loaded")
        s_mask = [sem(f"mask_loaded{j}") for j in range(4)]
        s_zero = sem("zeros_ready")
        s_zeroed = sem("sorted_zeroed")
        s_cast = sem("constants_cast")
        s_wq = sem("ternary_ready")
        s_wps = sem("weights_transposed")
        s_wsb = sem("weights_evacuated")
        s_amul = sem("a_exp_ready")
        s_a = sem("a_ready")
        s_ve = sem("variance_ready")
        s_lnv = sem("log_variance_ready")
        s_r0 = sem("rstd_guess")
        s_xn = sem("xn_ready")
        s_xnps = sem("xn_transposed")
        s_xnsb = sem("xnT_ready")
        s_xd = sem("projected")
        s_low = sem("xd_ready")
        s_bchi = sem("bc_high_ready")
        s_rest = sem("bc_rest_ready")
        s_bcmid = sem("bc_middle_ready")
        s_bclow = sem("bc_low_ready")
        s_bc3 = sem("bc3_ready")
        s_z = sem("z_ready")
        s_zb = sem("z_with_bias_ready")
        s_abs = sem("abs_ready")
        s_exp = sem("softplus_exp_ready")
        s_soft = sem("log1p_ready")
        s_delta = sem("delta_ready")
        s_u = sem("u_ready")
        s_diag = sem("diag_ready")
        s_dve = sem("dve_step")
        s_bready = sem("b_ready")
        s_cready = sem("c_ready")
        s_cevac = sem("c_evacuated")
        s_da = sem("decay_ready")
        s_bx = sem("bx_ready")
        s_scan = sem("scan_done")
        s_prod = sem("product_ready")
        s_sum = sem("product_summed")
        s_mps = sem("mask_transposed")
        s_wt = sem("mask_evacuated")
        s_wm = sem("expert_weights_ready")
        s_yT = sem("yT_ready")
        s_yps = sem("y_transposed")
        s_x1 = sem("x1_ready")
        s_xn2 = sem("xn2_ready")
        s_hi = sem("high_parts_ready")
        s_lo = sem("low_parts_ready")
        s_x2ps = sem("xn2_transposed")
        s_x2T = sem("xn2T_ready")
        s_lps = sem("logits_by_expert_ready")
        s_lsb = sem("logits_by_expert_evacuated")
        s_logit = sem("logits_ready")
        s_diff = sem("diff_ready")
        s_ex = sem("exp_ready")
        s_oh = sem("onehot_ready")
        s_rank = sem("ranks_ready")
        s_pos = sem("positions_ready")
        s_te = sem("tile_experts_ready")
        s_scat = sem("scattered")
        s_xs = [sem(f"sorted_loaded{j}") for j in range(4)]
        s_tps = sem("quad_transposed")
        s_tsb = sem("quad_evacuated")
        s_mm = sem("quad_multiplied")
        s_ysb = sem("quad_scaled")
        s_ys = [sem(f"quad_stored{j}") for j in range(2)]
        s_gath = [sem(f"gathered{q}") for q in range(4)]
        s_res = sem("result_ready")
        s_out = sem("result_stored")

        x_v = x.rearrange("b (t p) d -> p b t d", p=P)
        out_v = out.rearrange("b (t p) d -> p b t d", p=P)
        EARLY, LATE = 3, 4
        PEELED = 8
        Q4 = TB // 4
        y_bank = (4, 6, 0, 2)
        x2_bank = (4, 4, 4, 2)

        block = ctx.enter_context(nc.Block())

        @block.sync
        def _(sp):
            for q in range(4):
                sp.dma_start(x_sb[:, 4 * q:4 * q + 4, :], x_v[:, q // 2, 4 * (q % 2):4 * (q % 2) + 4, :]).then_inc(s_x[q], 16)
            sp.dma_start(w_nat[:, :, :], weight.rearrange("(h p) i -> p h i", p=P)).then_inc(s_late, 16)
            sp.dma_start(rw_nat[:, :], router_w).then_inc(s_late, 16)
            sp.dma_start(dsk[:, :], d_skip.rearrange("(h p) -> p h", p=P),
                         allow_slow_non_contiguous=True).then_inc(s_late, 16)
            sp.dma_start(scale_bc[:, :], scale.partition_broadcast(P)).then_inc(s_late, 16)
            sp.wait_ge(s_zero, 1)
            sp.wait_ge(s_scan, 1)
            sp.dma_start(xs.rearrange("(t p) c -> p t c", p=P),
                         zero[:, :].unsqueeze(1).to_broadcast([P, BLOCKS, 2 * D])).then_inc(s_zeroed, 16)

            def load_mask(e, j):
                sp.dma_start(mask_sb[:, j, :, :], masks[bass.ds(e, 1), :, :].rearrange("e (h p) i -> p (e h) i", p=P)
                             ).then_inc(s_mask[j], 16)

            for j in range(4):
                load_mask(j, j)
            with sp.Fori(1, E // 4) as i:
                for j in range(4):
                    sp.wait_ge(s_mps, i * 4 + (j - 3))
                    load_mask(i * 4 + j, j)
            xs_v = xs.rearrange("(g t p) c -> g p t c", t=4, p=P)
            ys_v = ys.rearrange("(q t p) d -> q p t d", t=4, p=M)

            def load(g, s):
                sp.dma_start(xs_sb[:, s, :, :], xs_v[bass.ds(g, 1)].rearrange("g p t c -> p (g t) c")).then_inc(s_xs[s], 16)

            def store(q, j, head=False):
                sp.wait_ge(s_ysb, q + 1)
                sp.dma_start(ys_v[bass.ds(q, 1)].rearrange("q p t d -> p (q t) d"), ys_sb[:, j, :, :]).then_inc(s_ys[j], 16)

            sp.wait_ge(s_scat, 16 * TB)
            for g in range(4):
                load(g, g)
            for q in range(QUADS // 2):
                if q % 2 == 0:
                    sp.wait_ge(s_tps, q + 2)
                    load(4 + q // 2, q // 2)
                store(q, q % 2)
            with sp.Fori(QUADS // 4, QUADS // 2) as i:
                for j in range(2):
                    store(i * 2 + j, j)
            for q in range(Q4):
                sp.wait_ge(s_res, 4 * q + 4)
                sp.dma_start(out_v[:, q // 2, 4 * (q % 2):4 * (q % 2) + 4, :], res[:, 4 * q:4 * q + 4, :]).then_inc(s_out, 16)
            sp.wait_ge(s_out, 16 * Q4)

        @block.gpsimd
        def _(pool):
            pool.memset(zero[:, :], 0.0).then_inc(s_zero, 1)

            def products(k, j, head=False):
                pool.wait_ge(s_cevac, k * 2 + 2)
                for dh in range(DH):
                    pool.wait_ge(s_scan, k * 2 + (dh + 1))
                    if not head:
                        pool.wait_ge(s_sum, k * 2 + (dh - 3))
                    pool.tensor_tensor(prod[:, j, dh, :], h[:, j, dh, :], cb[:, j, :], ALU.mult).then_inc(s_prod, 1)

            for j in range(2):
                products(j, j, head=True)
            with pool.Fori(1, B * N // 2) as i:
                for j in range(2):
                    products(i * 2 + j, j)

            for q in range(Q4):
                pool.wait_ge(s_hi, q + 1)
                pool.tensor_tensor(hl[:, 4 * q:4 * q + 4, D:2 * D], xn[:, 4 * q:4 * q + 4, :],
                                   hl[:, 4 * q:4 * q + 4, 0:D], ALU.subtract).then_inc(s_lo, 1)
            pool.wait_ge(s_zeroed, 16)
            pool.wait_ge(s_lo, Q4)
            pool.wait_ge(s_pos, 1)
            for t in range(TB):
                pool.indirect_dma_start(xs, bass.IndirectOffsetOnAxis(ap=pos[:, t:t + 1], axis=0),
                                        hl[:, t, :], None).then_inc(s_scat, 16)
            for j in range(2):
                pool.wait_ge(s_ys[j], 16 * (QUADS // 2))
            for t in range(TB):
                pool.indirect_dma_start(ytok[:, t, :], None, ys,
                                        bass.IndirectOffsetOnAxis(ap=pos[:, t:t + 1], axis=0)).then_inc(s_gath[t // 4], 16)

        @block.scalar
        def _(act):
            act.dma_start(cst[:, :], consts).then_inc(s_cst, 16)
            act.dma_start(wx_nat[:, :], w_xproj).then_inc(s_early, 16)
            act.dma_start(wd_nat[:, :, :], w_dt.rearrange("(h p) r -> p h r", p=P)).then_inc(s_early, 16)
            act.dma_start(bdt[:, :], b_dt.rearrange("(h p) -> p h", p=P),
                          allow_slow_non_contiguous=True).then_inc(s_early, 16)
            act.dma_start(alog[:, :, :], a_log.rearrange("(h p) n -> p h n", p=P)).then_inc(s_alog, 16)
            act.preload_act_table_set("natural_log_exp_and_others")
            def rstd_guess(n, blocks):
                act.wait_ge(s_ve, n)
                act.activation(lnv[:, blocks], ve[:, blocks], ACT.Ln).then_inc(s_lnv, 1)
                act.wait_ge(s_lnv, n)
                act.activation(r0[:, blocks], lnv[:, blocks], ACT.Exp, scale=-0.5).then_inc(s_r0, 1)

            def xnT_out(b, q, src):
                act.wait_ge(s_xnps, DH * LH * b + q + 1)
                dh, c = q % DH, q // DH
                act.activation(xnT[:, dh, b * L + c * HC:b * L + (c + 1) * HC], src, ACT.Copy).then_inc(s_xnsb, 1)

            def low_out(b, c, src):
                act.wait_ge(s_xd, LH * b + c + 1)
                if b:
                    act.wait_ge(s_z, DH * LH)
                    act.wait_ge(s_bc3, LH)
                act.activation(xd[:, c * HC:(c + 1) * HC], src[0:96, :], ACT.Copy).then_inc(s_low, 1)

            def soft_part(b, q, src):
                n = DH * LH * b + q
                bias = bdt[:, q % DH:q % DH + 1]
                act.wait_ge(s_z, n + 1)
                if b:
                    act.wait_ge(s_delta, DH * LH)
                act.activation(zb[:, q, :], src, ACT.Identity, bias=bias)
                act.activation(soft[:, q, :], src, ACT.Abs, bias=bias).then_inc(s_abs, 1)
                act.wait_ge(s_abs, n + 1)
                act.activation(soft[:, q, :], soft[:, q, :], ACT.Exp, scale=-1.0).then_inc(s_exp, 1)
                act.wait_ge(s_exp, n + 1)
                act.activation(soft[:, q, :], soft[:, q, :], ACT.Ln, bias=1.0).then_inc(s_soft, 1)

            lanes = slice(R, 96)

            def bc_high(c):
                act.wait_ge(s_low, LH + c + 1)
                act.activation(bc3[lanes, L + c * HC:L + (c + 1) * HC], xd[lanes, c * HC:(c + 1) * HC], ACT.Copy).then_inc(s_bchi, 1)

            def bc_middle(c):
                act.wait_ge(s_rest, c + 1)
                act.activation(bc_mid[lanes, c, :], bc_rest[lanes, c, :], ACT.Copy).then_inc(s_bcmid, 1)

            def bc_move(c):
                cols = slice(L + c * HC, L + (c + 1) * HC)
                act.wait_ge(s_bcmid, c + 1)
                act.activation(bc3[0:32, cols], bc_mid[lanes, c, :], ACT.Copy)
                act.wait_ge(s_bclow, c + 1)
                act.activation(bc3[32:64, cols], bc_low[lanes, c, :], ACT.Copy).then_inc(s_bc3, 1)

            rstd_guess(1, slice(0, LB))
            wd_ps, wx_ps, rw_ps = bank[0:R, 6, 0:D], bank[:, 6, D:D + DH * 96], bank[:, 6, HC - DH * E:HC]
            act.wait_ge(s_wps, 1)
            act.activation(wxT[:, :, :], wx_ps.rearrange("p (h k) -> p h k", h=DH), ACT.Copy).then_inc(s_wsb, 1)
            act.activation(wdT[:, :], wd_ps, ACT.Copy).then_inc(s_wsb, 1)
            rstd_guess(2, slice(LB, TB))
            for q in range(DH * LH):
                xnT_out(0, q, bank[:, q, :])
            act.wait_ge(s_alog, 16)
            act.activation(a_exp[:, :, :], alog[:, :, :], ACT.Exp).then_inc(s_amul, 1)
            for c in range(LH):
                low_out(0, c, bank[:, 4 + c, :])
            for q in range(DH * LH):
                soft_part(0, q, bank[:, q, :])
            act.wait_ge(s_wps, 2)
            act.activation(rwT[:, :, :], rw_ps.rearrange("p (h e) -> p h e", h=DH), ACT.Copy).then_inc(s_wsb, 1)
            act.activation(wqT[:, :, :], bank[:, 7, :].rearrange("p (h o) -> p h o", h=DH), ACT.Copy).then_inc(s_wsb, 1)

            act.wait_ge(s_a, 1)
            act.wait_ge(s_delta, DH * LH)

            def c_row(k, j, c, head=False):
                if not head and c == 0:
                    act.wait_ge(s_prod, k * 2 - 2)
                act.wait_ge(s_cready, k * 2 + (c + 1))
                act.activation(cb[:, j, c * HC:(c + 1) * HC], c_ps, ACT.Copy).then_inc(s_cevac, 1)

            def mask_out(e):
                act.wait_ge(s_mps, e + 1)
                act.activation(wT[:, bass.ds(e, 1), :, :].rearrange("p e h o -> p (e h o)"), w_ps, ACT.Copy).then_inc(s_wt, 1)

            def decays(b, n, k, j, head=False):
                for dh in range(DH):
                    if not head:
                        act.wait_ge(s_scan, k * 2 + (dh - 3))
                    act.activation(dA[:, j, dh, :], delta[:, dh, b * L:(b + 1) * L], ACT.Exp,
                                   scale=a_neg[:, dh, bass.ds(n, 1)]).then_inc(s_da, 1)

            def y_out(b):
                for dh in range(DH):
                    act.wait_ge(s_sum, DH * N * (b + 1) + dh - 1)
                    act.activation(yT[:, b, dh, :], yacc[:, dh, :], ACT.Copy).then_inc(s_yT, 1)

            def prepare(k):
                if k < 2:
                    for q in range(2 * k, 2 * k + 2):
                        xnT_out(1, q, w_ps)
                elif k == 2:
                    for c in range(LH):
                        low_out(1, c, w_ps)
                    for c in range(LH):
                        bc_high(c)
                elif k < 7:
                    soft_part(1, k - 3, w_ps)
                    if k == 3:
                        for c in range(LH):
                            bc_middle(c)
                    elif k < 6:
                        bc_move(k - 4)

            for k in range(PEELED):
                decays(0, k, k, k % 2, head=(k < 2))
                for c in range(LH):
                    c_row(k, k % 2, c, head=(k < 2))
                prepare(k)
            act.wait_ge(s_delta, B * DH * LH)
            act.wait_ge(s_bc3, B * LH)
            with act.Fori(PEELED // 2, N // 2) as i:
                for j in range(2):
                    decays(0, i * 2 + j, i * 2 + j, j)
                    for c in range(LH):
                        c_row(i * 2 + j, j, c)
                        mask_out(i * 4 + (2 * j + c - 2 * PEELED))

            def state_of_second(n, j):
                decays(1, n, n + N, j)
                c_row(n + N, j, 0)
                mask_out(n + N)
                c_row(n + N, j, 1)

            for n in range(2):
                state_of_second(n, n)
            y_out(0)
            with act.Fori(1, N // 2) as i:
                for j in range(2):
                    state_of_second(i * 2 + j, j)
            act.activation(ident16[:, :], ident, ACT.Copy).then_inc(s_cast, 1)
            act.activation(tri_bf[:, :], cst[:, C_TRI:C_TRI + P], ACT.Copy).then_inc(s_cast, 1)
            act.activation(ones_bf[:, :], cst[:, C_ONE:C_ONE + P], ACT.Copy).then_inc(s_cast, 1)
            rstd_guess(3, slice(0, LB))
            y_out(1)

            def logits_out(q):
                act.wait_ge(s_lps, q + 1)
                act.activation(logitsT[:, q * HC:(q + 1) * HC], bank[0:E, 6 + q % 2, :], ACT.Copy).then_inc(s_lsb, 1)

            for q in range(Q4):
                if q == 2:
                    rstd_guess(4, slice(LB, TB))
                act.wait_ge(s_xn2, 4 * q + 4)
                act.wait_ge(s_x2ps, q + 1)
                act.activation(xn2T[:, :, q * HC:(q + 1) * HC], bank[:, x2_bank[q]:x2_bank[q] + 2, :], ACT.Copy).then_inc(s_x2T, 1)
                act.activation(hl[:, 4 * q:4 * q + 4, 0:D], xn[:, 4 * q:4 * q + 4, :], ACT.Copy).then_inc(s_hi, 1)
                if q:
                    logits_out(q - 1)
            logits_out(Q4 - 1)
            act.wait_ge(s_diff, 1)
            act.activation(ex[:, :, :], diff[:, :, :], ACT.Exp).then_inc(s_ex, 1)

            def quad_out(q, j, head=False):
                act.wait_ge(s_tps, q + 1)
                if not head:
                    act.wait_ge(s_mm, q - 1)
                act.activation(xsT[:, j, :, :, :].rearrange("p b q t -> p (b q t)"), bank[:, j, :].bitcast(fp16),
                               ACT.Copy).then_inc(s_tsb, 1)

            quad_out(0, 0, head=True)
            quad_out(1, 1, head=True)
            with act.Fori(1, QUADS // 2) as i:
                for j in range(2):
                    quad_out(i * 2 + j, j)

        @block.vector
        def _(dve):
            step = [0]

            def then_next(ins):
                step[0] += 1
                ins.then_inc(s_dve, 1)
                dve.wait_ge(s_dve, step[0])

            def norm_stats(blocks):
                for t in range(blocks.start, blocks.stop):
                    if x_wait and t % 4 == 0:
                        dve.wait_ge(s_x[t // 4], 16)
                    last = dve.bn_stats(st[:, t, :], x_sb[:, t, :])
                then_next(last)
                for t in range(blocks.start, blocks.stop):
                    last = dve.bn_aggr(mv[:, t, :], st[:, t, :])
                then_next(last)
                dve.tensor_scalar(ve[:, blocks], mv[:, blocks, 1], EPS, None, ALU.add).then_inc(s_ve, 1)

            def norm_apply(n, blocks, done):
                dve.wait_ge(s_r0, n)
                then_next(dve.tensor_tensor(rr[:, blocks], r0[:, blocks], r0[:, blocks], ALU.mult))
                then_next(dve.tensor_tensor(rt[:, blocks], rr[:, blocks], ve[:, blocks], ALU.mult))
                then_next(dve.tensor_scalar(rr[:, blocks], rt[:, blocks], -0.5, 1.5, ALU.mult, ALU.add))
                then_next(dve.tensor_tensor(rstd[:, blocks], rr[:, blocks], r0[:, blocks], ALU.mult))
                for t in range(blocks.start, blocks.stop):
                    dve.tensor_scalar(xn[:, t, :], x_sb[:, t, :], mv[:, t, 0:1], rstd[:, t:t + 1],
                                      ALU.subtract, ALU.mult).then_inc(done, 1)

            lanes = slice(R, 96)

            def bc_parts(c):
                cols = slice(c * HC, (c + 1) * HC)
                dve.wait_ge(s_low, c + 1)
                then_next(dve.tensor_copy(bc3[lanes, cols], xd[lanes, cols]))
                then_next(dve.tensor_tensor(bc_rest[lanes, c, :], xd[lanes, cols], bc3[lanes, cols], ALU.subtract))
                then_next(dve.tensor_copy(bc_mid[lanes, c, :], bc_rest[lanes, c, :]))
                then_next(dve.tensor_tensor(bc_low[lanes, c, :], bc_rest[lanes, c, :], bc_mid[lanes, c, :], ALU.subtract))
                then_next(dve.tensor_copy(bc3[0:32, cols], bc_mid[lanes, c, :]))
                dve.tensor_copy(bc3[32:64, cols], bc_low[lanes, c, :]).then_inc(s_bc3, 1)
                dve.wait_ge(s_bc3, c + 1)

            def bc_subtract_high(c):
                dve.wait_ge(s_bchi, c + 1)
                dve.tensor_tensor(bc_rest[lanes, c, :], xd[lanes, c * HC:(c + 1) * HC], bc3[lanes, L + c * HC:L + (c + 1) * HC],
                                  ALU.subtract).then_inc(s_rest, 1)

            def bc_subtract_middle(c):
                dve.wait_ge(s_bcmid, c + 1)
                dve.tensor_tensor(bc_low[lanes, c, :], bc_rest[lanes, c, :], bc_mid[lanes, c, :], ALU.subtract).then_inc(s_bclow, 1)

            def delta_u(b, q):
                dh, c = q % DH, q // DH
                n, cols = DH * LH * b + q + 1, slice(b * L + c * HC, b * L + (c + 1) * HC)
                dve.wait_ge(s_soft, n)
                dve.scalar_tensor_tensor(delta[:, dh, cols], zb[:, q, :], 0.0, soft[:, q, :], ALU.max, ALU.add).then_inc(s_delta, 1)
                dve.wait_ge(s_delta, n)
                dve.tensor_tensor(u[:, dh, cols], delta[:, dh, cols], xnT[:, dh, cols], ALU.mult).then_inc(s_u, 1)

            x_wait = True
            norm_stats(slice(0, LB))
            norm_apply(1, slice(0, LB), s_xn)
            dve.wait_ge(s_cst, 16)
            then_next(dve.tensor_tensor(pick[:, :], ident[0:96, 0:32], ident[0:96, 32:64], ALU.add))
            dve.tensor_tensor(pick[:, :], pick[:, :], ident[0:96, 64:96], ALU.add).then_inc(s_diag, 1)
            norm_stats(slice(LB, TB))
            norm_apply(2, slice(LB, TB), s_xn)
            dve.wait_ge(s_amul, 1)
            dve.tensor_scalar(a_neg[:, :, :], a_exp[:, :, :], -1.0, None, ALU.mult).then_inc(s_a, 1)
            dve.wait_ge(s_late, 16 * LATE)
            then_next(dve.tensor_scalar(w_neg[:, :, :], w_nat[:, :, :], -0.25, None, ALU.is_lt))
            dve.scalar_tensor_tensor(w_nat[:, :, :], w_nat[:, :, :], 0.25, w_neg[:, :, :], ALU.is_gt, ALU.subtract).then_inc(s_wq, 1)
            for dh in range(DH):
                dve.tensor_scalar(diag_d[:, dh, :], ident, dsk[:, dh:dh + 1], None, ALU.mult).then_inc(s_diag, 1)
            for c in range(LH):
                bc_parts(c)
            for q in range(DH * LH):
                delta_u(0, q)

            def scans(b, k, j, head=False):
                rows = slice(b * L, (b + 1) * L)
                dve.wait_ge(s_bready, k + 1)
                for dh in range(DH):
                    if not (head and j == 0):
                        dve.wait_ge(s_scan, k * 2 + (dh - 1))
                    dve.tensor_tensor(bx[:, dh, :], b_ps, u[:, dh, rows], ALU.mult).then_inc(s_bx, 1)
                for dh in range(DH):
                    dve.wait_ge(s_bx, k * 2 + (dh + 1))
                    dve.wait_ge(s_da, k * 2 + (dh + 1))
                    if not head:
                        dve.wait_ge(s_prod, k * 2 + (dh - 3))
                    dve.tensor_tensor_scan(h[:, j, dh, :], dA[:, j, dh, :], bx[:, dh, :], 0.0,
                                           ALU.mult, ALU.add).then_inc(s_scan, 1)

            def prepare(k):
                if k == 2:
                    for c in range(LH):
                        bc_subtract_high(c)
                elif k >= 3:
                    if k == 3:
                        for c in range(LH):
                            bc_subtract_middle(c)
                    else:
                        delta_u(1, k - 4)

            dve.wait_ge(s_u, DH * LH)
            for k in range(PEELED):
                scans(0, k, k % 2, head=(k < 2))
                prepare(k)
            with dve.Fori(PEELED // 2, N // 2) as i:
                for j in range(2):
                    scans(0, i * 2 + j, j)
            dve.wait_ge(s_u, B * DH * LH)
            with dve.Fori(N // 2, N) as i:
                for j in range(2):
                    scans(1, i * 2 + j, j)

            x_wait = False
            for half in range(2):
                for g in range(2 * half, 2 * half + 2):
                    dve.wait_ge(s_yps, g + 1)
                    four = x_sb[:, 4 * g:4 * g + 4, :].rearrange("p t d -> p (t d)")
                    dve.tensor_tensor(four, bank[:, y_bank[g]:y_bank[g] + 2, :].rearrange("p c n -> p (c n)"), four, ALU.add).then_inc(s_x1, 1)
                dve.wait_ge(s_x1, 2 * half + 2)
                norm_stats(slice(half * LB, (half + 1) * LB))
                norm_apply(3 + half, slice(half * LB, (half + 1) * LB), s_xn2)
            logits = bank[:, 0, :].rearrange("p (t e) -> p t e", e=E)
            dve.wait_ge(s_logit, 1)
            then_next(dve.tensor_reduce(mx[:, :], logits, AX.X, ALU.max))
            dve.tensor_tensor(diff[:, :, :], logits, mx[:, :].unsqueeze(2).to_broadcast([P, TB, E]), ALU.subtract).then_inc(s_diff, 1)
            dve.wait_ge(s_diff, 1)
            from_end = cst[:, C_RE:C_RE + E].unsqueeze(1).to_broadcast([P, TB, E])
            then_next(dve.scalar_tensor_tensor(cand[:, :, :], diff[:, :, :], 0.0, from_end, ALU.is_equal, ALU.mult))
            then_next(dve.tensor_reduce(first[:, :], cand[:, :, :], AX.X, ALU.max))
            dve.tensor_tensor(oh[:, :, :], from_end, first[:, :].unsqueeze(2).to_broadcast([P, TB, E]), ALU.is_equal).then_inc(s_oh, 1)
            dve.wait_ge(s_ex, 1)
            then_next(dve.tensor_reduce(se[:, :], ex[:, :, :], AX.X, ALU.add))
            dve.reciprocal(top_w[:, :], se[:, :])
            dve.wait_ge(s_rank, 1)
            then_next(dve.tensor_scalar(cnt[:, :], bank[:, 6, 0:E], float(M - 1), None, ALU.add))
            then_next(dve.tensor_scalar(cnt_t[:, :], cnt[:, :], M.bit_length() - 1, None, ALU.arith_shift_right))
            then_next(dve.tensor_copy(ntile[:, :], cnt_t[:, :]))
            then_next(dve.tensor_tensor_scan(incl[:, :], cst[:, C_ONE:C_ONE + E], ntile[:, :], 0.0, ALU.mult, ALU.add))
            then_next(dve.tensor_tensor(base[:, :], incl[:, :], ntile[:, :], ALU.subtract))
            then_next(dve.scalar_tensor_tensor(where[:, :, :], base[:, :].unsqueeze(1).to_broadcast([P, TB, E]), float(M),
                                               bank[:, 5, :].rearrange("p (t e) -> p t e", e=E), ALU.mult, ALU.add))
            then_next(dve.tensor_tensor(where[:, :, :], where[:, :, :], oh[:, :, :], ALU.mult))
            then_next(dve.tensor_reduce(pos_f[:, :], where[:, :, :], AX.X, ALU.add))
            dve.tensor_copy(pos[:, :], pos_f[:, :]).then_inc(s_pos, 1)
            then_next(dve.tensor_tensor(past[:, :, :], incl[:, :].unsqueeze(1).to_broadcast([P, TILES, E]),
                                        cst[:, C_TILE:C_TILE + TILES].unsqueeze(2).to_broadcast([P, TILES, E]), ALU.is_le))
            then_next(dve.tensor_reduce(te_f[:, :], past[:, :, :], AX.X, ALU.add))
            dve.tensor_scalar(te[:, :], te_f[:, :], float(E - 1), None, ALU.min).then_inc(s_te, 1)
            dve.wait_ge(s_wt, E)
            dve.wait_ge(s_wsb, 4)
            for e in range(0, E, 8):
                eight = wT[:, e:e + 8, :, :].rearrange("p e h o -> p e (h o)")
                dve.tensor_tensor(eight, eight, wqT[:, :, :].rearrange("p h o -> p (h o)").unsqueeze(1).to_broadcast([P, 8, DH * D]),
                                  ALU.mult).then_inc(s_wm, 1)

            def scaled(q, j, stored=None):
                dve.wait_ge(s_mm, q + 1)
                if stored is not None:
                    dve.wait_ge(s_ys[j], stored)
                dve.tensor_tensor(ys_sb[:, j, :, :], bank[0:M, 2 + 2 * j:4 + 2 * j, :].rearrange("p c (t d) -> p (c t) d", d=D),
                                  scale_bc[0:M, :].unsqueeze(1).to_broadcast([M, 4, D]), ALU.mult).then_inc(s_ysb, 1)

            for j in range(2):
                scaled(j, j)
            with dve.Fori(1, QUADS // 2) as i:
                for j in range(2):
                    scaled(i * 2 + j, j, stored=i * 16)
            for t in range(TB):
                if t % 4 == 0:
                    dve.wait_ge(s_gath[t // 4], 16 * 4)
                dve.scalar_tensor_tensor(res[:, t, :], ytok[:, t, :], top_w[:, t:t + 1], x_sb[:, t, :],
                                         ALU.mult, ALU.add).then_inc(s_res, 1)

        @block.tensor
        def _(pe):
            wd_ps, wx_ps, rw_ps = bank[0:R, 6, 0:D], bank[:, 6, D:D + DH * 96], bank[:, 6, HC - DH * E:HC]
            pe.wait_ge(s_cst, 16)
            pe.wait_ge(s_early, 16 * EARLY)
            for dh in range(DH):
                pe.transpose(wx_ps[:, 96 * dh:96 * dh + 96], wx_nat[:, dh * P:(dh + 1) * P], ident[0:96, 0:96])
            for dh in range(DH):
                mm = pe.transpose(wd_ps[:, dh * P:(dh + 1) * P], wd_nat[:, dh, :], ident)
            mm.then_inc(s_wps, 1)

            def turn_xn(b, q, dst):
                dh, c = q % DH, q // DH
                for t in range(4):
                    blk = b * LB + 4 * c + t
                    pe.wait_ge(s_xn, blk + 1)
                    mm = pe.transpose(dst[:, t * P:(t + 1) * P], xn[:, blk, dh * P:(dh + 1) * P], ident)
                mm.then_inc(s_xnps, 1)

            def project(b, c, dst):
                cols = slice(b * L + c * HC, b * L + (c + 1) * HC)
                pe.wait_ge(s_xnsb, DH * LH * b + DH * (c + 1))
                for dh in range(DH):
                    mm = pe.matmul(dst[0:96, :], wxT[:, dh, :], xnT[:, dh, cols], start=(dh == 0), stop=(dh == DH - 1))
                mm.then_inc(s_xd, 1)

            def delta_in(b, q, dst):
                dh, c = q % DH, q // DH
                pe.wait_ge(s_low, LH * b + c + 1)
                pe.matmul(dst, wdT[:, dh * P:(dh + 1) * P], xd[0:R, c * HC:(c + 1) * HC], start=True, stop=True).then_inc(s_z, 1)

            for q in range(DH * LH):
                turn_xn(0, q, bank[:, q, :])
            pe.wait_ge(s_wsb, 2)
            for c in range(LH):
                project(0, c, bank[:, 4 + c, :])
            pe.wait_ge(s_xnsb, DH * LH)
            for q in range(DH * LH):
                delta_in(0, q, bank[:, q, :])
            pe.wait_ge(s_wq, 1)
            for dh in range(DH):
                pe.transpose(rw_ps[:, E * dh:E * dh + E], rw_nat[:, dh * P:(dh + 1) * P], ident[0:E, 0:E])
            for ic in range(DH):
                for oc in range(DH):
                    mm = pe.transpose(bank[:, 7, ic * D + oc * P:ic * D + (oc + 1) * P],
                                      w_nat[:, oc, ic * P:(ic + 1) * P], ident)
            mm.then_inc(s_wps, 1)

            def prepare(k, half):
                m = 2 * k + half
                if k < 2:
                    if m:
                        pe.wait_ge(s_xnsb, DH * LH + m)
                    else:
                        pe.wait_ge(s_wsb, 4)
                    turn_xn(1, m, w_ps)
                elif k == 2:
                    pe.wait_ge(s_xnsb, 2 * DH * LH)
                    if half == 1:
                        pe.wait_ge(s_low, LH + 1)
                    project(1, half, w_ps)
                elif k < 7 and half == 0:
                    q = k - 3
                    if q == 0:
                        pe.wait_ge(s_low, 2 * LH)
                    else:
                        pe.wait_ge(s_abs, DH * LH + q)
                    delta_in(1, q, w_ps)

            pe.wait_ge(s_diag, 1 + DH)
            pe.wait_ge(s_bc3, LH)
            pe.wait_ge(s_abs, DH * LH)
            pe.wait_ge(s_low, LH)

            def b_rows(b, n, k, head=False):
                if not head:
                    pe.wait_ge(s_bx, k * 2)
                for c in range(LH):
                    cols = slice(b * L + c * HC, b * L + (c + 1) * HC)
                    mm = pe.matmul(b_ps[:, c * HC:(c + 1) * HC], pick[:, bass.ds(n, 1)].to_broadcast([96, P]),
                                   bc3[:, cols], start=True, stop=True)
                mm.then_inc(s_bready, 1)

            def c_row(b, n, k, c, head=False):
                cols = slice(b * L + c * HC, b * L + (c + 1) * HC)
                if head and c == 0:
                    pe.wait_ge(s_wsb, 4)
                else:
                    pe.wait_ge(s_cevac, k * 2 + c)
                pe.matmul(c_ps, pick[:, bass.ds(n + N, 1)].to_broadcast([96, P]), bc3[:, cols],
                          start=True, stop=True).then_inc(s_cready, 1)

            def turn_mask(e, j, times, head=False):
                pe.wait_ge(s_mask[j], times)
                if head:
                    pe.wait_ge(s_abs, B * DH * LH)
                else:
                    pe.wait_ge(s_wt, e)
                for ic in range(DH):
                    for oc in range(DH):
                        mm = pe.transpose(w_ps[:, ic * D + oc * P:ic * D + (oc + 1) * P],
                                          mask_sb[:, j, oc, ic * P:(ic + 1) * P], ident)
                mm.then_inc(s_mps, 1)

            def skip_term(b, dh):
                for c in range(LH):
                    cols = slice(b * L + c * HC, b * L + (c + 1) * HC)
                    pe.matmul(yacc[:, dh, c * HC:(c + 1) * HC], diag_d[:, dh, :], xnT[:, dh, cols],
                              start=True, stop=False, skip_group_check=True)

            def sums(k, j, dh, last=False):
                pe.wait_ge(s_prod, k * 2 + (dh + 1))
                for c in range(LH):
                    mm = pe.matmul(yacc[:, dh, c * HC:(c + 1) * HC], ident, prod[:, j, dh, c * HC:(c + 1) * HC],
                                   start=False, stop=last, skip_group_check=True)
                mm.then_inc(s_sum, 1)

            for dh in range(DH):
                skip_term(0, dh)
            for k in range(PEELED + 2):
                b_rows(0, k, k, head=(k == 0))
                for c in range(LH):
                    c_row(0, k, k, c, head=(k == 0))
                    if k < PEELED:
                        prepare(k, c)
                    else:
                        e = 2 * (k - PEELED) + c
                        turn_mask(e, e, 16, head=(e == 0))
                    if k >= 2:
                        sums(k - 2, k % 2, c)
            with pe.Fori(PEELED // 2 + 1, N // 2) as i:
                for j in range(2):
                    b_rows(0, i * 2 + j, i * 2 + j)
                    for c in range(LH):
                        c_row(0, i * 2 + j, i * 2 + j, c)
                        turn_mask(i * 4 + (2 * j + c - 2 * PEELED), 2 * j + c, i * 16 - (8 * PEELED - 16))
                        sums(i * 2 + (j - 2), j, c)

            def state_of_second(n, slot, times, before=0, last=False):
                b_rows(1, n, n + N)
                for c in range(LH):
                    c_row(1, n, n + N, c)
                    if c == 0:
                        turn_mask(n + N, slot, times)
                    if before:
                        pe.wait_ge(s_yT, c + 1)
                        skip_term(1, c)
                    sums(n + (N - 2), slot % 2, c, last=last)

            FIRST = 16 * (N // 4 + 1)
            for n in range(4):
                state_of_second(n, n, FIRST, before=(n == 2), last=(n == 1))
            with pe.Fori(1, N // 4) as i:
                for n in range(4):
                    state_of_second(i * 4 + n, n, i * 16 + FIRST)

            def turn_y(g):
                for t in range(4):
                    for dh in range(DH):
                        blk = 4 * g + t
                        mm = pe.transpose(bank[:, y_bank[g] + t // 2, (t % 2) * D + dh * P:(t % 2) * D + (dh + 1) * P],
                                          yT[:, blk // LB, dh, (blk % LB) * P:(blk % LB + 1) * P], ident)
                mm.then_inc(s_yps, 1)

            pe.wait_ge(s_bx, B * N * DH)
            turn_y(0)
            pe.wait_ge(s_cevac, B * N * LH)
            pe.wait_ge(s_wt, E)
            turn_y(1)
            for j in range(2):
                for dh in range(DH):
                    sums(B * N - 2 + j, j, dh, last=(j == 1))
            pe.wait_ge(s_yT, DH * B)
            for g in range(2, Q4):
                turn_y(g)

            def turn_logits(q):
                pe.wait_ge(s_lsb, q + 1)
                for t in range(4 * q, 4 * q + 4):
                    mm = pe.transpose(bank[:, 0, t * E:(t + 1) * E], logitsT[:, t * P:(t + 1) * P], ident[0:E, 0:E])
                return mm

            for q in range(Q4 + 1):
                if q < Q4:
                    if q < 3:
                        pe.wait_ge(s_x1, 2)
                    else:
                        pe.wait_ge(s_x1, Q4)
                    if q:
                        pe.wait_ge(s_x2T, q)
                    for t in range(4):
                        pe.wait_ge(s_xn2, 4 * q + t + 1)
                        for dh in range(DH):
                            mm = pe.transpose(bank[:, x2_bank[q] + dh, t * P:(t + 1) * P],
                                              xn[:, 4 * q + t, dh * P:(dh + 1) * P], ident)
                    mm.then_inc(s_x2ps, 1)
                if q:
                    pe.wait_ge(s_x2T, q)
                    for dh in range(DH):
                        mm = pe.matmul(bank[0:E, 6 + (q - 1) % 2, :], rwT[:, dh, :], xn2T[:, dh, (q - 1) * HC:q * HC],
                                       start=(dh == 0), stop=(dh == DH - 1))
                    mm.then_inc(s_lps, 1)
            for q in range(Q4):
                mm = turn_logits(q)
            mm.then_inc(s_logit, 1)
            pe.wait_ge(s_oh, 1)
            pe.wait_ge(s_cast, 3)
            oh_f = oh[:, :, :].rearrange("p t e -> p (t e)")
            for t in range(TB):
                pe.matmul(bank[:, 6, 0:E], ones_bf[:, :], oh[:, t, :], start=(t == 0), stop=(t == TB - 1))
            pe.matmul(bank[:, 5, :], tri_bf[:, :], oh_f, start=True, stop=False, skip_group_check=True)
            for s in range(1, TB):
                mm = pe.matmul(bank[:, 5, s * E:], ones_bf[:, :], oh_f[:, 0:(TB - s) * E], start=False,
                               stop=(s == TB - 1), skip_group_check=True)
            mm.then_inc(s_rank, 1)

            pe.wait_ge(s_te, 1)
            pe.wait_ge(s_wm, E // 8)

            def turn(q, s, times, head=False):
                j = s % 2
                pe.wait_ge(s_xs[s // 2], times)
                if not head:
                    pe.wait_ge(s_tsb, q - 1)
                tps = bank[:, j, :].bitcast(fp16)
                for blk in range(2):
                    for part in range(4):
                        at = (4 * blk + part) * P
                        mm = pe.transpose(tps[:, at:at + P], xs_sb[:, s // 2, 2 * (s % 2) + blk, part * P:(part + 1) * P], ident16[:, :])
                mm.then_inc(s_tps, 1)

            def experts_of(q):
                _, experts = nc.values_load_multi_w_load_instructions(
                    te[0:1, bass.ds(q * 4, 4)], engines=[mybir.EngineType.PE], min_val=0, max_val=E - 1,
                    skip_runtime_bounds_check_because="VectorE takes the minimum with E - 1, and a count is not negative")
                return experts

            def multiply(q, j, experts, head=False):
                pe.wait_ge(s_tsb, q + 1)
                if not head:
                    pe.wait_ge(s_ysb, q - 1)
                for tile in range(4):
                    for part in range(4):
                        mm = pe.matmul(bank[0:M, 2 + 2 * j + tile // 2, (tile % 2) * D:(tile % 2 + 1) * D],
                                       xsT[:, j, tile // 2, part, (tile % 2) * M:(tile % 2 + 1) * M],
                                       wT[:, bass.ds(experts[tile], 1), part % 2, :].rearrange("p e o -> p (e o)"),
                                       start=(part == 0), stop=(part == 3))
                mm.then_inc(s_mm, 1)

            experts = [experts_of(q) for q in range(2)]
            for s in range(8):
                turn(s, s, 16, head=(s < 2))
                if s:
                    multiply(s - 1, (s - 1) % 2, experts[(s - 1) % 2], head=(s < 3))
                    experts[(s - 1) % 2] = experts_of(s + 1)
            with pe.Fori(1, QUADS // 8) as i:
                for s in range(8):
                    turn(i * 8 + s, s, i * 16 + 16)
                    multiply(i * 8 + (s - 1), (s - 1) % 2, experts_of(i * 8 + (s - 1)))
            multiply(QUADS - 1, 1, experts_of(QUADS - 1))


_INS = ['L0_attn_x', 'L0_attn_W_xproj', 'L0_attn_W_dt', 'L0_attn_b_dt', 'L0_attn_A_log', 'L0_attn_D',
        'L0_ffn_weight', 'L0_ffn_scale', 'L0_ffn_expert_masks', 'L0_ffn_router_w']


def _constants():
    import numpy as np
    c = np.zeros((P, C_END), np.float32)
    c[:, C_ID:C_ID + P] = np.eye(P)
    c[:, C_TRI:C_TRI + P] = np.triu(np.ones((P, P)), 1)
    c[:, C_ONE:C_ONE + P] = 1.0
    c[:, C_RE:C_RE + E] = E - np.arange(E)
    c[:, C_TILE:C_TILE + TILES] = np.arange(TILES)
    return c


def kernel(**inputs):
    import numpy as _np
    import concourse.bacc as _bacc
    from concourse import mybir as _mybir
    from concourse.bass_utils import run_bass_kernel_spmd as _run

    nc = _bacc.Bacc("TRN2", target_bir_lowering=False, num_devices=1)
    arrays, args = {}, []
    for name in _INS + ["constants"]:
        a = _constants() if name == "constants" else _np.ascontiguousarray(inputs[name])
        arrays[f"in_{name}_dram"] = a
        args.append(nc.dram_tensor(f"in_{name}_dram", a.shape, _mybir.dt.from_np(a.dtype), kind="ExternalInput").ap())
    args.append(nc.dram_tensor("out_0_dram", (B, L, D), _mybir.dt.float32, kind="ExternalOutput").ap())
    selective_scan_then_routed_ternary_ffn(nc, *args)
    r = _run(nc, [arrays], core_ids=[0])
    return r.results[0]["out_0_dram"]
```

```python
import concourse.bass as bass
from concourse import mybir
from contextlib import ExitStack

P = 128
B, L, D = 2, 1024, 256
R, N = 64, 16
E = 32
T = B * L
TB = T // P
LB = L // P
DH = D // P
HC = 512
LH = L // HC
M = 64
TILES = 64
SLOTS = TILES * M
BLOCKS = SLOTS // P
QUADS = TILES // 4
LOADS = QUADS // 2
ROW = 2 * D + 2
SKIP = 2 * T
EPS = 1e-5
C_ID, C_TRI, C_ONE, C_RE, C_TILE, C_GO, C_TOK, C_END = 0, 128, 256, 384, 416, 480, 992, 1008


def selective_scan_then_routed_ternary_ffn(nc, x, w_xproj, w_dt, b_dt, a_log, d_skip,
                                           weight, scale, masks, router_w, consts, out):
    fp32, fp16, bf16 = mybir.dt.float32, mybir.dt.float16, mybir.dt.bfloat16
    i32 = mybir.dt.int32
    ALU, ACT, AX = mybir.AluOpType, mybir.ActivationFunctionType, mybir.AxisListType

    xs = nc.dram_tensor("sorted_tokens", (SLOTS, ROW), fp32, kind="Internal").ap()

    ctx = ExitStack()
    with ctx:
        def sb(name, shape, dt=fp32):
            return ctx.enter_context(nc.sbuf_tensor(name, shape, dt))

        def sem(name):
            return ctx.enter_context(nc.semaphore(name))

        cst = sb("cst", [P, C_END])
        ident = cst[:, C_ID:C_ID + P]
        ident16 = sb("ident16", [P, P], fp16)
        ident_bf = sb("ident_bf", [P, P], bf16)
        tri_bf = sb("tri_bf", [P, P], bf16)
        ones_bf = sb("ones_bf", [P, P], bf16)
        pick = sb("pick", [96, E], bf16)
        x_sb = sb("x_sb", [P, TB, D])
        xn = sb("xn", [P, TB, D])
        xnT = sb("xnT", [P, DH, T])
        rows = sb("rows", [P, TB, ROW])
        delta_and_u = rows[:, :, :].rearrange("p t c -> p (t c)")
        delta = delta_and_u[:, 0:DH * T].rearrange("p (h l) -> p h l", h=DH)
        u = delta_and_u[:, DH * T:2 * DH * T].rearrange("p (h l) -> p h l", h=DH)
        yT = xn[:, :, :].rearrange("p t d -> p (t d)").rearrange("p (b h l) -> p b h l", b=B, h=DH)
        bdt = sb("bdt", [P, DH])
        dsk = sb("dsk", [P, DH])
        xd = sb("xd", [96, L])
        alog = sb("alog", [P, DH, N])
        a_exp = sb("a_exp", [P, DH, N])
        a_neg = sb("a_neg", [P, DH, N])
        scale_bc = sb("scale_bc", [P, D])
        wxT = sb("wxT", [P, DH, 96])
        wdT = sb("wdT", [R, D])
        rwT = sb("rwT", [P, DH, E])
        w_nat = sb("w_nat", [P, DH, D])
        wqT = sb("wqT", [P, DH, D], fp16)
        rw_nat = wqT[:, :, :].rearrange("p h o -> p (h o)").bitcast(fp32)[0:E, :]
        diag_d = sb("diag_d", [P, DH, P])
        bc3 = sb("bc3", [96, T], bf16)
        st = sb("st", [P, TB, 6])
        mv = sb("mv", [P, TB, 2])
        ve = sb("ve", [P, TB])
        lnv = sb("lnv", [P, TB])
        r0 = sb("r0", [P, TB])
        rr = sb("rr", [P, TB])
        rt = sb("rt", [P, TB])
        rstd = sb("rstd", [P, TB])
        dA = sb("dA", [P, 2, DH, L])
        bx = sb("bx", [P, DH, L])
        xs_sb = sb("xs_sb", [P, 4, 4, ROW])
        h_and_prod = xs_sb[:, :, :, :].rearrange("p s t c -> p (s t c)")
        h = h_and_prod[:, 0:2 * DH * L].rearrange("p (a h l) -> p a h l", a=2, h=DH)
        prod = h_and_prod[:, 2 * DH * L:4 * DH * L].rearrange("p (a h l) -> p a h l", a=2, h=DH)
        cb = sb("cb", [P, 2, L])
        mask_sb = sb("mask_sb", [P, 4, DH, D])
        mask_upper = mask_sb[:, :, :, :].bitcast(bf16).rearrange("p j h (i w) -> p j h i w", w=2)[:, :, :, :, 1]
        wT = sb("wT", [P, E, DH, D], fp16)

        flat = "p a h l -> p (a h l)"
        before = prod[:, :, :, :].rearrange(flat)
        wx_nat = before[0:96, 1024:1024 + D]
        wd_nat = before[:, 1536:1536 + DH * R].rearrange("p (h r) -> p h r", h=DH)
        early = wT[:, :, :, :].rearrange("p e h o -> p (e h o)").bitcast(fp32)
        zb = early[:, 0:4 * HC].rearrange("p (q c) -> p q c", q=4)
        soft = early[:, 4 * HC:8 * HC].rearrange("p (q c) -> p q c", q=4)
        bc_rest = early[:, 8 * HC:10 * HC].rearrange("p (c n) -> p c n", c=LH)
        bc_mid = early[:, 10 * HC:11 * HC].bitcast(bf16).rearrange("p (c n) -> p c n", c=LH)
        bc_low = early[:, 11 * HC:12 * HC].bitcast(bf16).rearrange("p (c n) -> p c n", c=LH)
        w_neg, w_pos = (early[:, n * HC:(n + 1) * HC].rearrange("p (h i) -> p h i", h=DH) for n in range(12, 14))
        after = dA[:, :, :, :].rearrange(flat)
        diff, ex, cand, where = (after[:, n * TB * E:(n + 1) * TB * E].rearrange("p (t e) -> p t e", t=TB)
                                 for n in range(4))
        upto = cand.rearrange("p t e -> p (t e)")
        past = after[:, 4 * TB * E:4 * TB * E + TILES * E].rearrange("p (t e) -> p t e", e=E)
        xsT = xn[:, :, :].rearrange("p t d -> p (t d)")[:, 0:2 * 2 * 4 * 3 * M // 2].bitcast(fp16).rearrange(
            "p (j b q t) -> p j b q t", j=2, b=2, q=4)
        xsT_tiles = xsT.rearrange("p j b q (s t) -> p j (b q) s t", t=M)
        y_sb = cb[:, :, :].rearrange("p j (q t d) -> p (j q) t d", t=2, d=D)
        high_low = rows[:, :, 0:D].bitcast(fp16)
        x1 = rows[:, :, D:2 * D]
        top_w, token = rows[:, :, 2 * D], rows[:, :, 2 * D + 1]
        xn2T = prod[:, :, :, :].rearrange(flat).rearrange("p (h l) -> p h l", h=DH)
        mx = sb("mx", [P, TB])
        se = sb("se", [P, TB])
        spare = bx[:, 1, L // 2:L]
        first = sb("first", [P, TB])
        oh = spare[:, 0:TB * E // 2].bitcast(bf16).rearrange("p (t e) -> p t e", t=TB)
        cnt, cnt_t, ntile, incl, base = (spare[:, TB * E // 2 + n * E:TB * E // 2 + (n + 1) * E] for n in range(5))
        cnt, cnt_t = cnt.bitcast(i32), cnt_t.bitcast(i32)
        pos_f = sb("pos_f", [P, TB])
        pos = sb("pos", [P, TB], i32)
        te_f = bx[:, 0, L // 2:L // 2 + TILES]
        te = sb("te", [P, TILES], i32)
        no_token = sb("no_token", [P, 8])
        to_token = sb("to_token", [P, 8], i32)
        zero = sb("zero", [P, ROW // 2])

        bank = ctx.enter_context(nc.psum_tensor("bank", [P, 8, HC], fp32))
        yacc = bank[:, 0:4, :].rearrange("p (h c) n -> p h (c n)", h=DH)
        b_ps = bank[:, 4:6, :].rearrange("p c n -> p (c n)")
        c_ps = bank[:, 6, :]
        w_ps = bank[:, 7, :]
        last_mask_ps = [bank[:, 1 + n, 0:DH * D // 2].bitcast(bf16) for n in range(2)]
        rw_ps = bank[:, 6, 0:DH * E]
        mask_ps = w_ps[:, 0:DH * D // 2].bitcast(bf16)

        s_x = [sem(f"x_loaded{q}") for q in range(4)]
        s_cst = sem("constants_loaded")
        s_early = sem("early_weights_loaded")
        s_alog = sem("a_log_loaded")
        s_late = sem("late_weights_loaded")
        s_mask = [sem(f"mask_loaded{j}") for j in range(4)]
        s_zero = sem("zeros_ready")
        s_zeroed = sem("sorted_zeroed")
        s_cast = sem("constants_cast")
        s_wq = sem("ternary_ready")
        s_wps = sem("weights_transposed")
        s_wsb = sem("weights_evacuated")
        s_w2 = sem("second_layer_weights_evacuated")
        s_amul = sem("a_exp_ready")
        s_a = sem("a_ready")
        s_ve = sem("variance_ready")
        s_lnv = sem("log_variance_ready")
        s_r0 = sem("rstd_guess")
        s_rstd = sem("rstd_ready")
        s_xn = sem("xn_ready")
        s_xnpool = sem("xn_ready_from_gpsimd")
        s_xnps = sem("xn_transposed")
        s_xnsb = sem("xnT_ready")
        s_xd = sem("projected")
        s_low = sem("xd_ready")
        s_bchi = sem("bc_high_ready")
        s_rest = sem("bc_rest_ready")
        s_bcmid = sem("bc_middle_ready")
        s_bclow = sem("bc_low_ready")
        s_bc3 = sem("bc3_ready")
        s_z = sem("z_ready")
        s_abs = sem("abs_ready")
        s_exp = sem("softplus_exp_ready")
        s_soft = sem("log1p_ready")
        s_delta = sem("delta_ready")
        s_u = sem("u_ready")
        s_diag = sem("diag_ready")
        s_pick = sem("pick_ready")
        s_idbf = sem("bf16_identity_ready")
        s_sign = sem("weight_signs_ready")
        s_dve = sem("dve_step")
        s_bready = sem("b_ready")
        s_cready = sem("c_ready")
        s_cevac = sem("c_evacuated")
        s_da = sem("decay_ready")
        s_bx = sem("bx_ready")
        s_scan = sem("scan_done")
        s_prod = sem("product_ready")
        s_sum = sem("product_summed")
        s_mps = sem("mask_transposed")
        s_wt = sem("mask_evacuated")
        s_wm = sem("expert_weights_ready")
        s_yT = sem("yT_ready")
        s_yps = sem("y_transposed")
        s_x1 = sem("x1_ready")
        s_xn2 = sem("xn2_ready")
        s_hi = sem("high_parts_ready")
        s_lo = sem("low_parts_ready")
        s_x2ps = sem("xn2_transposed")
        s_x2T = sem("xn2T_ready")
        s_logit = sem("logits_ready")
        s_diff = sem("diff_ready")
        s_ex = sem("exp_ready")
        s_oh = sem("onehot_ready")
        s_inblk = sem("ranks_in_expert_ready")
        s_rank = sem("ranks_ready")
        s_pos = sem("positions_ready")
        s_te = sem("tile_experts_ready")
        s_scat = sem("scattered")
        s_xs = [sem(f"sorted_loaded{j}") for j in range(4)]
        s_xs0 = sem("first_quad_loaded")
        s_tps = sem("quad_transposed")
        s_tsb = sem("quad_evacuated")
        s_mm = sem("quad_multiplied")
        s_none = sem("no_token_found")
        s_to = sem("to_token_ready")
        s_ysb = sem("tiles_scaled")
        s_fin = sem("block_finished")
        s_out = [sem(f"quad_sent{f}") for f in range(4)]
        s_pad = sem("padding_zeroed")
        s_topw = sem("softmax_weights_ready")

        x_v = x.rearrange("b (t p) d -> p b t d", p=P)
        out_v = out.rearrange("b l d -> (b l) d")
        EARLY, LATE = 3, 4
        lanes = slice(R, 96)
        PEELED = 8
        BESIDE = B * N - PEELED + 1
        PROMPT = 2
        POOLED = TB - 4
        Q4 = TB // 4
        y_bank = (4, 6, 0, 2)
        x2_bank = (4, 4, 4, 2)

        block = ctx.enter_context(nc.Block())

        @block.sync
        def _(sp):
            for q in range(4):
                sp.dma_start(x_sb[:, 4 * q:4 * q + 4, :], x_v[:, q // 2, 4 * (q % 2):4 * (q % 2) + 4, :]).then_inc(s_x[q], 16)
            sp.dma_start(w_nat[:, :, :], weight.rearrange("(h p) i -> p h i", p=P)).then_inc(s_late, 16)
            sp.dma_start(rw_nat[:, :], router_w).then_inc(s_late, 16)
            sp.dma_start(dsk[:, :], d_skip.rearrange("(h p) -> p h", p=P),
                         allow_slow_non_contiguous=True).then_inc(s_late, 16)
            sp.dma_start(scale_bc[:, :], scale.partition_broadcast(P)).then_inc(s_late, 16)
            sp.wait_ge(s_zero, 1)
            sp.wait_ge(s_scan, 1)
            sp.dma_start(xs.rearrange("(p t) (a c) -> p (t a) c", p=P, a=2),
                         zero[:, :].unsqueeze(1).to_broadcast([P, BLOCKS * 2, ROW // 2])).then_inc(s_zeroed, 16)

            def load_mask(e, j):
                sp.dma_start(mask_sb[:, j, :, :], masks[bass.ds(e, 1), :, :].rearrange("e (h p) i -> p (e h) i", p=P)
                             ).then_inc(s_mask[j], 16)

            for j in range(4):
                load_mask(j, j)
            with sp.Fori(1, E // 4) as i:
                for j in range(4):
                    sp.wait_ge(s_mps, i * 4 + (j - 3))
                    load_mask(i * 4 + j, j)
            xs_v = xs.rearrange("(g t p) c -> g p t c", t=4, p=P)
            sp.wait_ge(s_scat, 16 * TB)
            for g in range(LOADS):
                if g >= 4:
                    sp.wait_ge(s_tps, 2 * g - 6)
                    sp.wait_ge(s_fin, 4 * g - 12)
                if g == 0:
                    sp.dma_start(xs_sb[:, 0, 0:2, :], xs_v[0, :, 0:2, :]).then_inc(s_xs0, 16)
                    sp.dma_start(xs_sb[:, 0, 2:4, :], xs_v[0, :, 2:4, :]).then_inc(s_xs[0], 16)
                else:
                    sp.dma_start(xs_sb[:, g % 4, :, :], xs_v[g]).then_inc(s_xs[g % 4], 16)

        @block.gpsimd
        def _(pool):
            pool.memset(zero[:, :], 0.0).then_inc(s_zero, 1)

            pool.wait_ge(s_late, 16 * LATE)
            pool.wait_ge(s_cst, 16)
            pool.tensor_scalar(w_neg[:, :, :], w_nat[:, :, :], -0.25, None, ALU.is_lt).then_inc(s_sign, 1)
            pool.tensor_scalar(w_pos[:, :, :], w_nat[:, :, :], 0.25, None, ALU.is_gt).then_inc(s_sign, 1)
            pool.wait_ge(s_sign, 2)
            pool.tensor_tensor(w_nat[:, :, :], w_pos[:, :, :], w_neg[:, :, :], ALU.subtract).then_inc(s_wq, 1)
            for dh in range(DH):
                pool.tensor_scalar(diag_d[:, dh, :], ident, dsk[:, dh:dh + 1], None, ALU.mult).then_inc(s_diag, 1)

            pool.wait_ge(s_rstd, 2)
            for t in range(POOLED, TB):
                pool.tensor_scalar(xn[:, t, :], x_sb[:, t, :], mv[:, t, 0:1], rstd[:, t:t + 1],
                                   ALU.subtract, ALU.mult).then_inc(s_xnpool, 1)

            def products(k, j, head=False):
                pool.wait_ge(s_cevac, k * 2 + 2)
                for dh in range(DH):
                    pool.wait_ge(s_scan, k * 2 + (dh + 1))
                    if not head:
                        pool.wait_ge(s_sum, k * 2 + (dh - 3))
                    pool.tensor_tensor(prod[:, j, dh, :], h[:, j, dh, :], cb[:, j, :], ALU.mult).then_inc(s_prod, 1)

            def bc_subtract_high(c):
                pool.wait_ge(s_bchi, c + 1)
                pool.tensor_tensor(bc_rest[lanes, c, :], xd[lanes, c * HC:(c + 1) * HC], bc3[lanes, L + c * HC:L + (c + 1) * HC],
                                   ALU.subtract).then_inc(s_rest, 1)
                pool.wait_ge(s_rest, c + 1)

            def bc_subtract_middle(c):
                pool.wait_ge(s_bcmid, c + 1)
                pool.tensor_tensor(bc_low[lanes, c, :], bc_rest[lanes, c, :], bc_mid[lanes, c, :], ALU.subtract).then_inc(s_bclow, 1)
                pool.wait_ge(s_bclow, c + 1)

            for k in range(PEELED):
                products(k, k % 2, head=(k < 2))
                if 1 <= k < 4:
                    pool.wait_ge(s_prod, 2 * k + 2)
                if 2 <= k < 4:
                    bc_subtract_middle(k - 2)
                if 1 <= k < 3:
                    bc_subtract_high(k - 1)
            with pool.Fori(PEELED // 2, B * N // 2) as i:
                for j in range(2):
                    products(i * 2 + j, j)

            for q in range(Q4):
                pool.wait_ge(s_hi, q + 1)
                pool.tensor_tensor(high_low[:, 4 * q:4 * q + 4, D:2 * D], xn[:, 4 * q:4 * q + 4, :],
                                   high_low[:, 4 * q:4 * q + 4, 0:D], ALU.subtract).then_inc(s_lo, 1)
            pool.wait_ge(s_x2ps, Q4)
            pool.wait_ge(s_hi, Q4)
            pool.wait_ge(s_lo, Q4)
            pool.memset(xsT_tiles[:, :, :, 1, :].rearrange("p j a t -> p (j a) t"), 0.0).then_inc(s_pad, 1)
            pool.wait_ge(s_zeroed, 16)
            pool.wait_ge(s_lo, Q4)
            pool.wait_ge(s_topw, 2)
            for t in range(TB):
                if t == 0 or t == PROMPT:
                    pool.wait_ge(s_pos, 1 if t == 0 else 2)
                pool.indirect_dma_start(xs, bass.IndirectOffsetOnAxis(ap=pos[:, t:t + 1], axis=0),
                                        rows[:, t, :], None).then_inc(s_scat, 16)

            for q in range(QUADS):
                f = q % 4
                for blk in range(2):
                    pool.wait_ge(s_fin, q * 2 + (blk + 1))
                    pool.indirect_dma_start(out_v, bass.IndirectOffsetOnAxis(ap=to_token[:, 2 * f + blk:2 * f + blk + 1], axis=0),
                                            y_sb[:, f, blk, :], None, bounds_check=T - 1, oob_is_err=False).then_inc(s_out[f], 16)

            for f in range(4):
                pool.wait_ge(s_out[f], 32 * (QUADS // 4))

        @block.scalar
        def _(act):
            act.dma_start(cst[:, :], consts).then_inc(s_cst, 16)
            act.dma_start(wx_nat[:, :], w_xproj).then_inc(s_early, 16)
            act.dma_start(wd_nat[:, :, :], w_dt.rearrange("(h p) r -> p h r", p=P)).then_inc(s_early, 16)
            act.dma_start(bdt[:, :], b_dt.rearrange("(h p) -> p h", p=P),
                          allow_slow_non_contiguous=True).then_inc(s_early, 16)
            act.dma_start(alog[:, :, :], a_log.rearrange("(h p) n -> p h n", p=P)).then_inc(s_alog, 16)
            act.preload_act_table_set("natural_log_exp_and_others")
            def rstd_guess(n, blocks):
                act.wait_ge(s_ve, n)
                act.activation(lnv[:, blocks], ve[:, blocks], ACT.Ln).then_inc(s_lnv, 1)
                act.wait_ge(s_lnv, n)
                act.activation(r0[:, blocks], lnv[:, blocks], ACT.Exp, scale=-0.5).then_inc(s_r0, 1)

            def xnT_out(b, q, src):
                act.wait_ge(s_xnps, DH * LH * b + q + 1)
                dh, c = q % DH, q // DH
                act.activation(xnT[:, dh, b * L + c * HC:b * L + (c + 1) * HC], src, ACT.Copy).then_inc(s_xnsb, 1)

            def low_out(b, c, src):
                act.wait_ge(s_xd, LH * b + c + 1)
                if b:
                    act.wait_ge(s_z, DH * LH)
                    act.wait_ge(s_bc3, LH)
                act.activation(xd[:, c * HC:(c + 1) * HC], src[0:96, :], ACT.Copy).then_inc(s_low, 1)

            def soft_part(b, q, src):
                n = DH * LH * b + q
                bias = bdt[:, q % DH:q % DH + 1]
                act.wait_ge(s_z, n + 1)
                if b:
                    act.wait_ge(s_delta, DH * LH)
                act.activation(zb[:, q, :], src, ACT.Identity, bias=bias)
                act.activation(soft[:, q, :], src, ACT.Abs, bias=bias).then_inc(s_abs, 1)
                act.wait_ge(s_abs, n + 1)
                act.activation(soft[:, q, :], soft[:, q, :], ACT.Exp, scale=-1.0).then_inc(s_exp, 1)
                act.wait_ge(s_exp, n + 1)
                act.activation(soft[:, q, :], soft[:, q, :], ACT.Ln, bias=1.0).then_inc(s_soft, 1)

            def bc_move(q, part):
                src = (bc_mid, bc_low)[part][lanes, :, :].rearrange("p c n -> p (c n)")
                act.activation(bc3[32 * part:32 * part + 32, bass.ds(q * (L // 4) + L, L // 4)],
                               src[:, bass.ds(q * (L // 4), L // 4)], ACT.Copy).then_inc(s_bc3, 1)

            rstd_guess(1, slice(0, LB))
            wd_ps, wx_ps = bank[0:R, 6, 0:D], bank[:, 6, D:D + DH * 96]
            act.wait_ge(s_wps, 1)
            act.activation(wxT[:, :, :], wx_ps.rearrange("p (h k) -> p h k", h=DH), ACT.Copy).then_inc(s_wsb, 1)
            act.activation(wdT[:, :], wd_ps, ACT.Copy).then_inc(s_wsb, 1)
            for q in range(DH * LH):
                xnT_out(0, q, bank[:, q, :])
            act.wait_ge(s_alog, 16)
            act.activation(a_exp[:, :, :], alog[:, :, :], ACT.Exp).then_inc(s_amul, 1)
            low_out(0, 0, bank[:, 4, :])
            rstd_guess(2, slice(LB, TB))
            low_out(0, 1, bank[:, 5, :])
            for q in range(DH * LH):
                soft_part(0, q, bank[:, q, :])
            for q in range(DH * LH):
                xnT_out(1, q, bank[:, 4 + q, :])
            act.wait_ge(s_a, 1)
            act.wait_ge(s_delta, DH * LH)

            def c_row(k, j, c, head=False):
                if not head and c == 0:
                    act.wait_ge(s_prod, k * 2 - 2)
                act.wait_ge(s_cready, k * 2 + (c + 1))
                act.activation(cb[:, j, c * HC:(c + 1) * HC], c_ps, ACT.Copy).then_inc(s_cevac, 1)

            def mask_out(e, src=mask_ps):
                act.wait_ge(s_mps, e + 1)
                act.activation(wT[:, bass.ds(e, 1), :, :].rearrange("p e h o -> p (e h o)"), src, ACT.Copy).then_inc(s_wt, 1)

            def decay(b, n, k, j, dh, head=False):
                if not head:
                    act.wait_ge(s_scan, k * 2 + (dh - 3))
                act.activation(dA[:, j, dh, :], delta[:, dh, b * L:(b + 1) * L], ACT.Exp,
                               scale=a_neg[:, dh, bass.ds(n, 1)]).then_inc(s_da, 1)

            def y_out(dh):
                act.wait_ge(s_sum, DH * N + dh - 1)
                act.activation(yT[:, 0, dh, :], yacc[:, dh, :], ACT.Copy).then_inc(s_yT, 1)

            def prepare(k):
                if k < 2:
                    low_out(1, k, w_ps)
                elif k < 6:
                    soft_part(1, k - 2, w_ps)

            for k in range(PEELED):
                for c in range(LH):
                    c_row(k, k % 2, c, head=(k < 2))
                    decay(0, k, k, k % 2, c, head=(k < 2))
                prepare(k)
            act.wait_ge(s_delta, B * DH * LH)
            mask_out(0)
            act.wait_ge(s_bcmid, LH)
            act.wait_ge(s_bclow, LH)
            with act.Fori(PEELED // 2, N // 2) as i:
                for j in range(2):
                    for c in range(LH):
                        c_row(i * 2 + j, j, c)
                        if c == 0:
                            mask_out(i * 2 + (j + 1 - PEELED))
                        decay(0, i * 2 + j, i * 2 + j, j, c)
                    bc_move(i - PEELED // 2, j)
            act.wait_ge(s_bc3, LH + 8)

            def state_of_second(n, j):
                c_row(n + N, j, 0)
                mask_out(n + (N - PEELED + 1))
                decay(1, n, n + N, j, 0)
                c_row(n + N, j, 1)
                decay(1, n, n + N, j, 1)

            for n in range(2):
                state_of_second(n, n)
            y_out(0)
            c_row(N + 2, 0, 0)
            y_out(1)
            mask_out(2 + N - PEELED + 1)
            c_row(N + 2, 0, 1)
            decay(1, 2, N + 2, 0, 0)
            decay(1, 2, N + 2, 0, 1)
            state_of_second(3, 1)
            with act.Fori(2, N // 2) as i:
                for j in range(2):
                    state_of_second(i * 2 + j, j)
            act.activation(ident16[:, :], ident, ACT.Copy).then_inc(s_cast, 1)
            act.activation(tri_bf[:, :], cst[:, C_TRI:C_TRI + P], ACT.Copy).then_inc(s_cast, 1)
            act.activation(ones_bf[:, :], cst[:, C_ONE:C_ONE + P], ACT.Copy).then_inc(s_cast, 1)
            rstd_guess(3, slice(0, LB))

            act.wait_ge(s_wps, 2)
            act.activation(rwT[:, :, :], rw_ps.rearrange("p (h e) -> p h e", h=DH), ACT.Copy).then_inc(s_w2, 1)
            act.activation(wqT[:, :, :], w_ps.rearrange("p (h o) -> p h o", h=DH), ACT.Copy).then_inc(s_w2, 1)

            def xn2T_out(q):
                act.wait_ge(s_x2ps, q + 1)
                act.activation(xn2T[:, :, q * HC:(q + 1) * HC], bank[:, x2_bank[q]:x2_bank[q] + 2, :], ACT.Copy).then_inc(s_x2T, 1)

            def high_part(q):
                act.wait_ge(s_xn2, 4 * q + 4)
                act.activation(high_low[:, 4 * q:4 * q + 4, 0:D], xn[:, 4 * q:4 * q + 4, :], ACT.Copy).then_inc(s_hi, 1)

            for q in range(2):
                xn2T_out(q)
                high_part(q)
            rstd_guess(4, slice(LB, TB))
            for q in range(2, Q4):
                xn2T_out(q)
            for q in range(2, Q4):
                high_part(q)
            for half in range(2):
                t = slice(half * LB, (half + 1) * LB)
                act.wait_ge(s_diff, half + 1)
                act.activation(ex[:, t, :], diff[:, t, :], ACT.Exp).then_inc(s_ex, 1)
            for e in range(BESIDE, E):
                mask_out(e, last_mask_ps[e % 2])

            def quad_out(q, j, head=False):
                act.wait_ge(s_tps, q + 1)
                if not head:
                    act.wait_ge(s_mm, q - 1)
                act.activation(xsT_tiles[:, j, :, 0::2, :], bank[:, j, :].bitcast(fp16).rearrange("p (a s t) -> p a s t", s=2, t=M),
                               ACT.Copy).then_inc(s_tsb, 1)

            act.wait_ge(s_pad, 1)
            quad_out(0, 0, head=True)
            quad_out(1, 1, head=True)
            with act.Fori(1, QUADS // 2) as i:
                for j in range(2):
                    quad_out(i * 2 + j, j)

        @block.vector
        def _(dve):
            step = [0]

            def then_next(ins):
                step[0] += 1
                ins.then_inc(s_dve, 1)
                dve.wait_ge(s_dve, step[0])

            def norm_stats(blocks, src=x_sb, between=None):
                for t in range(blocks.start, blocks.stop):
                    if x_wait and t % 4 == 0:
                        dve.wait_ge(s_x[t // 4], 16)
                    last = dve.bn_stats(st[:, t, :], src[:, t, :])
                then_next(last)
                if between is not None:
                    between(0)
                for t in range(blocks.start, blocks.stop):
                    last = dve.bn_aggr(mv[:, t, :], st[:, t, :])
                then_next(last)
                dve.tensor_scalar(ve[:, blocks], mv[:, blocks, 1], EPS, None, ALU.add).then_inc(s_ve, 1)
                if between is not None:
                    between(1)

            def norm_apply(n, blocks, done, src=x_sb, apply=None):
                dve.wait_ge(s_r0, n)
                then_next(dve.tensor_tensor(rr[:, blocks], r0[:, blocks], r0[:, blocks], ALU.mult))
                then_next(dve.tensor_tensor(rt[:, blocks], rr[:, blocks], ve[:, blocks], ALU.mult))
                then_next(dve.tensor_scalar(rr[:, blocks], rt[:, blocks], -0.5, 1.5, ALU.mult, ALU.add))
                dve.tensor_tensor(rstd[:, blocks], rr[:, blocks], r0[:, blocks], ALU.mult).then_inc(s_rstd, 1)
                dve.wait_ge(s_rstd, n)
                for t in range(blocks.start, blocks.stop if apply is None else apply):
                    dve.tensor_scalar(xn[:, t, :], src[:, t, :], mv[:, t, 0:1], rstd[:, t:t + 1],
                                      ALU.subtract, ALU.mult).then_inc(done, 1)

            def bc_parts():
                half = [slice(c * HC, (c + 1) * HC) for c in range(LH)]
                steps = (lambda c: dve.tensor_copy(bc3[lanes, half[c]], xd[lanes, half[c]]),
                         lambda c: dve.tensor_tensor(bc_rest[lanes, c, :], xd[lanes, half[c]], bc3[lanes, half[c]], ALU.subtract),
                         lambda c: dve.tensor_copy(bc_mid[lanes, c, :], bc_rest[lanes, c, :]),
                         lambda c: dve.tensor_tensor(bc_low[lanes, c, :], bc_rest[lanes, c, :], bc_mid[lanes, c, :], ALU.subtract),
                         lambda c: dve.tensor_copy(bc3[0:32, half[c]], bc_mid[lanes, c, :]))
                for n, one in enumerate(steps):
                    for c in range(LH):
                        if n:
                            dve.wait_ge(s_dve, step[0] - 1)
                        else:
                            dve.wait_ge(s_low, c + 1)
                        one(c).then_inc(s_dve, 1)
                        step[0] += 1
                for c in range(LH):
                    dve.wait_ge(s_dve, step[0] - 1 + c)
                    dve.tensor_copy(bc3[32:64, half[c]], bc_low[lanes, c, :]).then_inc(s_bc3, 1)

            def bc_high(c):
                dve.wait_ge(s_low, LH + c + 1)
                dve.tensor_copy(bc3[lanes, L + c * HC:L + (c + 1) * HC], xd[lanes, c * HC:(c + 1) * HC]).then_inc(s_bchi, 1)

            def bc_middle(c):
                dve.wait_ge(s_rest, c + 1)
                dve.tensor_copy(bc_mid[lanes, c, :], bc_rest[lanes, c, :]).then_inc(s_bcmid, 1)

            def delta_u(b, q):
                dh, c = q % DH, q // DH
                n, cols = DH * LH * b + q + 1, slice(b * L + c * HC, b * L + (c + 1) * HC)
                dve.wait_ge(s_soft, n)
                dve.scalar_tensor_tensor(delta[:, dh, cols], zb[:, q, :], 0.0, soft[:, q, :], ALU.max, ALU.add).then_inc(s_delta, 1)
                dve.wait_ge(s_delta, n)
                dve.tensor_tensor(u[:, dh, cols], delta[:, dh, cols], xnT[:, dh, cols], ALU.mult).then_inc(s_u, 1)

            x_wait = True
            norm_stats(slice(0, LB))
            norm_apply(1, slice(0, LB), s_xn)
            dve.wait_ge(s_cst, 16)
            then_next(dve.tensor_tensor(pick[:, :], ident[0:96, 0:32], ident[0:96, 32:64], ALU.add))
            dve.tensor_tensor(pick[:, :], pick[:, :], ident[0:96, 64:96], ALU.add).then_inc(s_pick, 1)
            dve.tensor_copy(ident_bf[:, :], ident).then_inc(s_idbf, 1)
            norm_stats(slice(LB, TB))
            norm_apply(2, slice(LB, TB), s_xn, apply=POOLED)
            dve.wait_ge(s_amul, 1)
            dve.tensor_scalar(a_neg[:, :, :], a_exp[:, :, :], -1.0, None, ALU.mult).then_inc(s_a, 1)
            bc_parts()
            for q in range(DH * LH):
                delta_u(0, q)

            def scans(b, k, j, head=False, between=None):
                rows = slice(b * L, (b + 1) * L)
                dve.wait_ge(s_bready, k + 1)
                for dh in range(DH):
                    if not (head and j == 0):
                        dve.wait_ge(s_scan, k * 2 + (dh - 1))
                    dve.tensor_tensor(bx[:, dh, :], b_ps, u[:, dh, rows], ALU.mult).then_inc(s_bx, 1)
                if between is not None:
                    delta_u(1, between)
                for dh in range(DH):
                    dve.wait_ge(s_bx, k * 2 + (dh + 1))
                    dve.wait_ge(s_da, k * 2 + (dh + 1))
                    if not head:
                        dve.wait_ge(s_prod, k * 2 + (dh - 3))
                    dve.tensor_tensor_scan(h[:, j, dh, :], dA[:, j, dh, :], bx[:, dh, :], 0.0,
                                           ALU.mult, ALU.add).then_inc(s_scan, 1)

            def prepare(k):
                if 2 <= k < 4:
                    bc_middle(k - 2)
                if 1 <= k < 3:
                    bc_high(k - 1)

            dve.wait_ge(s_u, DH * LH)
            for k in range(PEELED):
                scans(0, k, k % 2, head=(k < 2), between=k - 3 if 3 <= k < 7 else None)
                prepare(k)
            with dve.Fori(PEELED // 2, N // 2) as i:
                for j in range(2):
                    scans(0, i * 2 + j, j)
            dve.wait_ge(s_u, B * DH * LH)
            with dve.Fori(N // 2, N) as i:
                for j in range(2):
                    scans(1, i * 2 + j, j)

            def y_out_with_skip(dh):
                dve.wait_ge(s_sum, DH * N * B + dh - 1)
                dve.scalar_tensor_tensor(yT[:, 1, dh, :], xnT[:, dh, L:2 * L], dsk[:, dh:dh + 1], yacc[:, dh, :],
                                         ALU.mult, ALU.add).then_inc(s_yT, 1)

            x_wait = False
            for half in range(2):
                for g in range(2 * half, 2 * half + 2):
                    dve.wait_ge(s_yps, g + 1)
                    four = slice(4 * g, 4 * g + 4)
                    dve.tensor_tensor(x1[:, four, :], bank[:, y_bank[g]:y_bank[g] + 2, :].rearrange("p c (t d) -> p (c t) d", d=D),
                                      x_sb[:, four, :], ALU.add).then_inc(s_x1, 1)
                dve.wait_ge(s_x1, 2 * half + 2)
                norm_stats(slice(half * LB, (half + 1) * LB), x1, between=None if half else y_out_with_skip)
                norm_apply(3 + half, slice(half * LB, (half + 1) * LB), s_xn2, x1)
            for half in range(2):
                t = slice(half * LB, (half + 1) * LB)
                logits = bank[:, 6 + half, 0:LB * E].rearrange("p (t e) -> p t e", e=E)
                from_end = cst[:, C_RE:C_RE + E].unsqueeze(1).to_broadcast([P, LB, E])
                dve.wait_ge(s_logit, half + 1)
                then_next(dve.tensor_reduce(mx[:, t], logits, AX.X, ALU.max))
                dve.tensor_tensor(diff[:, t, :], logits, mx[:, t].unsqueeze(2).to_broadcast([P, LB, E]), ALU.subtract).then_inc(s_diff, 1)
                dve.wait_ge(s_diff, half + 1)
                then_next(dve.scalar_tensor_tensor(cand[:, t, :], diff[:, t, :], 0.0, from_end, ALU.is_equal, ALU.mult))
                then_next(dve.tensor_reduce(first[:, t], cand[:, t, :], AX.X, ALU.max))
                dve.tensor_tensor(oh[:, t, :], from_end, first[:, t].unsqueeze(2).to_broadcast([P, LB, E]), ALU.is_equal).then_inc(s_oh, 1)
            for half in range(2):
                t = slice(half * LB, (half + 1) * LB)
                dve.wait_ge(s_ex, half + 1)
                then_next(dve.tensor_reduce(se[:, t], ex[:, t, :], AX.X, ALU.add))
                dve.reciprocal(top_w[:, t], se[:, t])
                dve.tensor_copy(token[:, t], cst[:, C_TOK + half * LB:C_TOK + (half + 1) * LB]).then_inc(s_topw, 1)
            dve.wait_ge(s_rank, 1)
            then_next(dve.tensor_tensor_scan(upto[:, :], cst[:, C_GO:C_GO + E * TB], bank[:, 6, :], 0.0, ALU.mult, ALU.add))
            then_next(dve.tensor_scalar(cnt[:, :], upto[:, TB - 1::TB], float(M - 1), None, ALU.add))
            dve.tensor_tensor(where[:, :, :], bank[:, 5, :].rearrange("p (t e) -> p t e", e=E),
                              upto[:, :].rearrange("p (e t) -> p t e", e=E), ALU.add).then_inc(s_inblk, 1)
            then_next(dve.tensor_scalar(cnt_t[:, :], cnt[:, :], M.bit_length() - 1, None, ALU.arith_shift_right))
            then_next(dve.tensor_copy(ntile[:, :], cnt_t[:, :]))
            then_next(dve.tensor_tensor_scan(incl[:, :], cst[:, C_ONE:C_ONE + E], ntile[:, :], 0.0, ALU.mult, ALU.add))
            then_next(dve.tensor_tensor(base[:, :], incl[:, :], ntile[:, :], ALU.subtract))
            dve.wait_ge(s_inblk, 1)
            for t in (slice(0, PROMPT), slice(PROMPT, TB)):
                then_next(dve.scalar_tensor_tensor(where[:, t, :], base[:, :].unsqueeze(1).to_broadcast([P, t.stop - t.start, E]),
                                                   float(M), where[:, t, :], ALU.mult, ALU.add))
                then_next(dve.tensor_tensor(where[:, t, :], where[:, t, :], oh[:, t, :], ALU.mult))
                then_next(dve.tensor_reduce(pos_f[:, t], where[:, t, :], AX.X, ALU.add))
                dve.tensor_copy(pos[:, t], pos_f[:, t]).then_inc(s_pos, 1)
            then_next(dve.tensor_tensor(past[:, :, :], incl[:, :].unsqueeze(1).to_broadcast([P, TILES, E]),
                                        cst[:, C_TILE:C_TILE + TILES].unsqueeze(2).to_broadcast([P, TILES, E]), ALU.is_le))
            then_next(dve.tensor_reduce(te_f[:, :], past[:, :, :], AX.X, ALU.add))
            dve.tensor_scalar(te[:, :], te_f[:, :], float(E - 1), None, ALU.min).then_inc(s_te, 1)
            dve.wait_ge(s_wt, E)
            dve.wait_ge(s_w2, 2)
            for e in range(0, E, 8):
                eight = wT[:, e:e + 8, :, :].rearrange("p e h o -> p e (h o)")
                dve.tensor_tensor(eight, eight, wqT[:, :, :].rearrange("p h o -> p (h o)").unsqueeze(1).to_broadcast([P, 8, DH * D]),
                                  ALU.mult).then_inc(s_wm, 1)

            def finish(q, s, times, sent=None):
                f, rows_of = s % 4, xs_sb[:, s // 2, 2 * (s % 2):2 * (s % 2) + 2, :]
                here = slice(2 * f, 2 * f + 2)
                dve.wait_ge(s_xs0 if s == 0 and sent is None else s_xs[s // 2], times)
                if sent is not None:
                    dve.wait_ge(s_out[f], sent)
                dve.tensor_scalar(no_token[:, here], rows_of[:, :, 2 * D + 1], 0.0, float(SKIP), ALU.is_equal, ALU.mult).then_inc(s_none, 1)
                dve.wait_ge(s_mm, q + 1)
                dve.tensor_tensor(y_sb[:, f, :, :], bank[:, 2 + f, :].rearrange("p (t d) -> p t d", t=2),
                                  scale_bc[:, :].unsqueeze(1).to_broadcast([P, 2, D]), ALU.mult).then_inc(s_ysb, 1)
                dve.wait_ge(s_none, q + 1)
                dve.scalar_tensor_tensor(to_token[:, here], no_token[:, here], -1.0, rows_of[:, :, 2 * D + 1],
                                         ALU.add, ALU.add).then_inc(s_to, 1)
                dve.wait_ge(s_ysb, q + 1)
                dve.wait_ge(s_to, q + 1)
                for blk in range(2):
                    dve.scalar_tensor_tensor(y_sb[:, f, blk, :], y_sb[:, f, blk, :], rows_of[:, blk, 2 * D:2 * D + 1],
                                             rows_of[:, blk, D:2 * D], ALU.mult, ALU.add).then_inc(s_fin, 1)

            for s in range(8):
                finish(s, s, 16, sent=32 if s >= 4 else None)
            with dve.Fori(1, QUADS // 8) as i:
                for s in range(8):
                    finish(i * 8 + s, s, i * 16 + 16, sent=i * 64 + 32 * (s // 4))

        @block.tensor
        def _(pe):
            wd_ps, wx_ps = bank[0:R, 6, 0:D], bank[:, 6, D:D + DH * 96]
            pe.wait_ge(s_cst, 16)
            pe.wait_ge(s_early, 16 * EARLY)
            for dh in range(DH):
                pe.transpose(wx_ps[:, 96 * dh:96 * dh + 96], wx_nat[:, dh * P:(dh + 1) * P], ident[0:96, 0:96])
            for dh in range(DH):
                mm = pe.transpose(wd_ps[:, dh * P:(dh + 1) * P], wd_nat[:, dh, :], ident)
            mm.then_inc(s_wps, 1)

            def turn_xn(b, q, dst):
                dh, c = q % DH, q // DH
                for t in range(4):
                    blk = b * LB + 4 * c + t
                    if blk < POOLED:
                        pe.wait_ge(s_xn, blk + 1)
                    else:
                        pe.wait_ge(s_xnpool, blk - POOLED + 1)
                    mm = pe.transpose(dst[:, t * P:(t + 1) * P], xn[:, blk, dh * P:(dh + 1) * P], ident)
                mm.then_inc(s_xnps, 1)

            def project(b, c, dst):
                cols = slice(b * L + c * HC, b * L + (c + 1) * HC)
                pe.wait_ge(s_xnsb, DH * LH * b + DH * (c + 1))
                for dh in range(DH):
                    mm = pe.matmul(dst[0:96, :], wxT[:, dh, :], xnT[:, dh, cols], start=(dh == 0), stop=(dh == DH - 1))
                mm.then_inc(s_xd, 1)

            def delta_in(b, q, dst):
                dh, c = q % DH, q // DH
                pe.wait_ge(s_low, LH * b + c + 1)
                pe.matmul(dst, wdT[:, dh * P:(dh + 1) * P], xd[0:R, c * HC:(c + 1) * HC], start=True, stop=True).then_inc(s_z, 1)

            for q in range(DH * LH):
                turn_xn(0, q, bank[:, q, :])
            pe.wait_ge(s_wsb, 2)
            for c in range(LH):
                project(0, c, bank[:, 4 + c, :])
            pe.wait_ge(s_xnsb, DH * LH)
            for q in range(DH * LH):
                delta_in(0, q, bank[:, q, :])
            pe.wait_ge(s_low, LH)
            pe.wait_ge(s_wsb, 2)
            for q in range(DH):
                turn_xn(1, q, bank[:, 4 + q, :])

            def prepare(k, half):
                if k < 2 and half == 1:
                    if k == 0:
                        pe.wait_ge(s_xnsb, 2 * DH * LH)
                    else:
                        pe.wait_ge(s_low, LH + 1)
                    project(1, k, w_ps)
                elif 2 <= k < 6 and half == 1:
                    q = k - 2
                    if q == 0:
                        pe.wait_ge(s_low, 2 * LH)
                    else:
                        pe.wait_ge(s_abs, DH * LH + q)
                    delta_in(1, q, w_ps)
                elif k == PEELED - 1 and half == 1:
                    turn_mask(0, 0, 16, head=True)

            pe.wait_ge(s_pick, 1)
            pe.wait_ge(s_idbf, 1)
            pe.wait_ge(s_diag, DH)

            def b_rows(b, n, k, head=False):
                if not head:
                    pe.wait_ge(s_bx, k * 2)
                for c in range(LH):
                    cols = slice(b * L + c * HC, b * L + (c + 1) * HC)
                    mm = pe.matmul(b_ps[:, c * HC:(c + 1) * HC], pick[:, bass.ds(n, 1)].to_broadcast([96, P]),
                                   bc3[:, cols], start=True, stop=True)
                mm.then_inc(s_bready, 1)

            def c_row(b, n, k, c, head=False):
                cols = slice(b * L + c * HC, b * L + (c + 1) * HC)
                if head and c == 0:
                    pe.wait_ge(s_xnsb, DH * LH + 3)
                else:
                    pe.wait_ge(s_cevac, k * 2 + c)
                pe.matmul(c_ps, pick[:, bass.ds(n + N, 1)].to_broadcast([96, P]), bc3[:, cols],
                          start=True, stop=True).then_inc(s_cready, 1)

            def turn_mask(e, j, times, head=False, dst=mask_ps, left=0):
                pe.wait_ge(s_mask[j], times)
                if head:
                    pe.wait_ge(s_abs, B * DH * LH)
                else:
                    pe.wait_ge(s_wt, e - left)
                for ic in range(DH):
                    for oc in range(DH):
                        mm = pe.transpose(dst[:, ic * D + oc * P:ic * D + (oc + 1) * P],
                                          mask_upper[:, j, oc, ic * P:(ic + 1) * P], ident_bf[:, :])
                mm.then_inc(s_mps, 1)

            def skip_term(dh):
                for c in range(LH):
                    pe.wait_ge(s_abs, LH * dh + c + 1)
                    pe.matmul(yacc[:, dh, c * HC:(c + 1) * HC], diag_d[:, dh, :], xnT[:, dh, c * HC:(c + 1) * HC],
                              start=True, stop=False, skip_group_check=True)

            def sums(k, j, dh, first=False, last=False):
                pe.wait_ge(s_prod, k * 2 + (dh + 1))
                for c in range(LH):
                    mm = pe.matmul(yacc[:, dh, c * HC:(c + 1) * HC], ident, prod[:, j, dh, c * HC:(c + 1) * HC],
                                   start=first, stop=last, skip_group_check=True)
                mm.then_inc(s_sum, 1)

            skip_term(0)
            for q in range(DH, DH * LH):
                turn_xn(1, q, bank[:, 4 + q, :])
            skip_term(1)
            pe.wait_ge(s_bc3, LH)
            pe.wait_ge(s_xnsb, DH * LH + 2)
            for k in range(PEELED):
                b_rows(0, k, k, head=(k == 0))
                for c in range(LH):
                    c_row(0, k, k, c, head=(k == 0))
                    prepare(k, c)
                    if k >= 2:
                        sums(k - 2, k % 2, c)
            with pe.Fori(PEELED // 4, N // 4) as i:
                for j in range(4):
                    b_rows(0, i * 4 + j, i * 4 + j)
                    c_row(0, i * 4 + j, i * 4 + j, 0)
                    turn_mask(i * 4 + (j + 1 - PEELED), (j + 1) % 4, i * 16 + (16 * ((j + 1) // 4 + 1) - 4 * PEELED))
                    sums(i * 4 + (j - 2), j % 2, 0)
                    c_row(0, i * 4 + j, i * 4 + j, 1)
                    sums(i * 4 + (j - 2), j % 2, 1)

            def state_of_second(n, slot, times, before=False, after=False, last=False):
                e = n + (N - PEELED + 1)
                if not after:
                    b_rows(1, n, n + N)
                    c_row(1, n, n + N, 0)
                turn_mask(e, (slot + 1) % 4, times)
                if before:
                    c_row(1, n, n + N, 1)
                    for dh in range(DH):
                        pe.wait_ge(s_yT, dh + 1)
                        sums(n + (N - 2), slot % 2, dh, first=True)
                        if dh == 0:
                            b_rows(1, n + 1, n + N + 1)
                            c_row(1, n + 1, n + N + 1, 0)
                else:
                    sums(n + (N - 2), slot % 2, 0, last=last)
                    c_row(1, n, n + N, 1)
                    sums(n + (N - 2), slot % 2, 1, last=last)

            FIRST = 16 * ((N - PEELED) // 4 + 1)
            pe.wait_ge(s_bc3, LH + 8)
            for n in range(4):
                state_of_second(n, n, FIRST + 16 * ((n + 1) // 4), before=(n == 2), after=(n == 3), last=(n == 1))
            with pe.Fori(1, N // 4) as i:
                for n in range(4):
                    state_of_second(i * 4 + n, n, i * 16 + (FIRST + 16 * ((n + 1) // 4)))

            def turn_y(g):
                for t in range(4):
                    for dh in range(DH):
                        blk = 4 * g + t
                        mm = pe.transpose(bank[:, y_bank[g] + t // 2, (t % 2) * D + dh * P:(t % 2) * D + (dh + 1) * P],
                                          yT[:, blk // LB, dh, (blk % LB) * P:(blk % LB + 1) * P], ident)
                mm.then_inc(s_yps, 1)

            pe.wait_ge(s_bx, B * N * DH)
            turn_y(0)
            pe.wait_ge(s_cevac, B * N * LH)
            pe.wait_ge(s_wt, BESIDE)
            turn_y(1)
            for j in range(2):
                for dh in range(DH):
                    sums(B * N - 2 + j, j, dh, last=(j == 1))
            pe.wait_ge(s_x1, 2)
            pe.wait_ge(s_wq, 1)
            for dh in range(DH):
                pe.transpose(rw_ps[:, E * dh:E * dh + E], rw_nat[:, dh * P:(dh + 1) * P], ident[0:E, 0:E])
            for ic in range(DH):
                for oc in range(DH):
                    mm = pe.transpose(w_ps[:, ic * D + oc * P:ic * D + (oc + 1) * P],
                                      w_nat[:, oc, ic * P:(ic + 1) * P], ident)
            mm.then_inc(s_wps, 1)
            pe.wait_ge(s_yT, DH * B)
            for g in range(2, Q4):
                turn_y(g)

            def keep_clock(n, dst):
                for _ in range(n):
                    pe.matmul(dst, ident16[:, :], wT[:, 0, :, :].rearrange("p h o -> p (h o)"), start=True, stop=True)

            pe.wait_ge(s_cast, 1)
            def turn_xn2(q):
                for t in range(4):
                    pe.wait_ge(s_xn2, 4 * q + t + 1)
                    for dh in range(DH):
                        mm = pe.transpose(bank[:, x2_bank[q] + dh, t * P:(t + 1) * P],
                                          xn[:, 4 * q + t, dh * P:(dh + 1) * P], ident)
                mm.then_inc(s_x2ps, 1)

            def logits(q):
                pe.wait_ge(s_x2T, q + 1)
                for t in range(4 * q, 4 * q + 4):
                    for dh in range(DH):
                        mm = pe.matmul(bank[:, 6 + t // LB, (t % LB) * E:(t % LB + 1) * E], xn2T[:, dh, t * P:(t + 1) * P],
                                       rwT[:, dh, :], start=(dh == 0), stop=(dh == DH - 1))
                return mm

            turn_xn2(0)
            pe.wait_ge(s_x2T, 1)
            turn_xn2(1)
            pe.wait_ge(s_w2, DH)
            logits(0)
            logits(1).then_inc(s_logit, 1)
            pe.wait_ge(s_x1, Q4)
            keep_clock(12, bank[:, 0, :])
            turn_xn2(2)
            turn_xn2(3)
            logits(2)
            logits(3).then_inc(s_logit, 1)
            keep_clock(8, bank[:, 0, :])
            pe.wait_ge(s_oh, 2)
            pe.wait_ge(s_cast, 3)
            oh_f = oh[:, :, :].rearrange("p t e -> p (t e)")
            pe.matmul(bank[:, 6, :].rearrange("p (e t) -> p e t", e=E), ones_bf[:, :], oh[:, :, :].rearrange("p t e -> p e t"),
                      start=True, stop=True)
            pe.matmul(bank[:, 5, :], tri_bf[:, :], oh_f, start=True, stop=True).then_inc(s_rank, 1)
            for e in range(BESIDE, E):
                turn_mask(e, e % 4, 16 * (e // 4 + 1), dst=last_mask_ps[e % 2], left=1)

            pe.wait_ge(s_te, 1)
            pe.wait_ge(s_wm, E // 8)

            def turn(q, s, times, head=False):
                j = s % 2
                pe.wait_ge(s_xs0 if s == 0 and head else s_xs[s // 2], times)
                if not head:
                    pe.wait_ge(s_tsb, q - 1)
                tps = bank[:, j, :].bitcast(fp16)
                parts = xs_sb[:, s // 2, 2 * (s % 2):2 * (s % 2) + 2, 0:D].bitcast(fp16)
                for blk in range(2):
                    for part in range(4):
                        at = (4 * blk + part) * P
                        mm = pe.transpose(tps[:, at:at + P], parts[:, blk, part * P:(part + 1) * P], ident16[:, :])
                mm.then_inc(s_tps, 1)

            def experts_of(q):
                _, experts = nc.values_load_multi_w_load_instructions(
                    te[0:1, bass.ds(q * 4, 4)], engines=[mybir.EngineType.PE], min_val=0, max_val=E - 1,
                    skip_runtime_bounds_check_because="VectorE takes the minimum with E - 1, and a count is not negative")
                return experts

            def multiply(q, f, experts, head=False):
                pe.wait_ge(s_tsb, q + 1)
                if not head:
                    pe.wait_ge(s_ysb, q - 3)
                for tile in range(4):
                    blk, odd = tile // 2, tile % 2
                    for part in range(4):
                        mm = pe.matmul(bank[:, 2 + f, blk * D:(blk + 1) * D],
                                       xsT[:, f % 2, blk, part, odd * M:odd * M + P],
                                       wT[:, bass.ds(experts[tile], 1), part % 2, :].rearrange("p e o -> p (e o)"),
                                       start=(odd == 0 and part == 0), stop=(odd == 1 and part == 3))
                mm.then_inc(s_mm, 1)

            experts = [experts_of(q) for q in range(2)]
            keep_clock(14, w_ps)
            for s in range(8):
                turn(s, s, 16, head=(s < 2))
                if s:
                    multiply(s - 1, (s - 1) % 4, experts[(s - 1) % 2], head=(s < 5))
                    experts[(s - 1) % 2] = experts_of(s + 1)
            with pe.Fori(1, QUADS // 8) as i:
                for s in range(8):
                    turn(i * 8 + s, s, i * 16 + 16)
                    multiply(i * 8 + (s - 1), (s - 1) % 4, experts_of(i * 8 + (s - 1)))
            multiply(QUADS - 1, 3, experts_of(QUADS - 1))


_INS = ['L0_attn_x', 'L0_attn_W_xproj', 'L0_attn_W_dt', 'L0_attn_b_dt', 'L0_attn_A_log', 'L0_attn_D',
        'L0_ffn_weight', 'L0_ffn_scale', 'L0_ffn_expert_masks', 'L0_ffn_router_w']


def _constants():
    import numpy as np
    c = np.zeros((P, C_END), np.float32)
    c[:, C_ID:C_ID + P] = np.eye(P)
    c[:, C_TRI:C_TRI + P] = np.triu(np.ones((P, P)), 1) - 1
    c[:, C_ONE:C_ONE + P] = 1.0
    c[:, C_RE:C_RE + E] = E - np.arange(E)
    c[:, C_TILE:C_TILE + TILES] = np.arange(TILES)
    c[:, C_GO:C_GO + E * TB] = np.arange(E * TB) % TB > 0
    c[:, C_TOK:C_TOK + TB] = 1 + np.arange(P)[:, None] + P * np.arange(TB)
    return c


def kernel(**inputs):
    import numpy as _np
    import concourse.bacc as _bacc
    from concourse import mybir as _mybir
    from concourse.bass_utils import run_bass_kernel_spmd as _run

    nc = _bacc.Bacc("TRN2", target_bir_lowering=False, num_devices=1)
    arrays, args = {}, []
    for name in _INS + ["constants"]:
        a = _constants() if name == "constants" else _np.ascontiguousarray(inputs[name])
        arrays[f"in_{name}_dram"] = a
        args.append(nc.dram_tensor(f"in_{name}_dram", a.shape, _mybir.dt.from_np(a.dtype), kind="ExternalInput").ap())
    args.append(nc.dram_tensor("out_0_dram", (B, L, D), _mybir.dt.float32, kind="ExternalOutput").ap())
    selective_scan_then_routed_ternary_ffn(nc, *args)
    r = _run(nc, [arrays], core_ids=[0])
    return r.results[0]["out_0_dram"]
```
